# Optimizing a Trainium2 kernel written in Bass

```python
import numpy as np
import jax
import jax.numpy as jnp

def _softmax(x, axis=-1):
    return jax.nn.softmax(x, axis=axis)

def _gelu(x):
    return jax.nn.gelu(x, approximate=True)

def _silu(x):
    return jax.nn.silu(x)

def _sigmoid(x):
    return jax.nn.sigmoid(x)

def _layernorm(x, axis=-1, eps=1e-05):
    m = jnp.mean(x, axis=axis, keepdims=True)
    v = jnp.var(x, axis=axis, keepdims=True)
    return (x - m) / jnp.sqrt(v + eps)

def _scatter_add(tgt, idx, src, axis=0):
    return tgt.at[idx].add(src)

def _segment_sum(src, seg, n):
    return jax.ops.segment_sum(src, seg, n)
kernel_name = 'mk_xattn_ffn_d1_seqx_r8_9f8753'

def setup_inputs(seed: int=0):
    np.random.seed(seed)
    _w = jnp.asarray

    def _rec_inputs():
        import jax
        import jax.numpy as jnp
        _rk = jax.random.key(seed)
        x = -0.0003929 + 0.9999 * jax.random.normal(jax.random.fold_in(_rk, 1), (8, 256, 128), jnp.float32)
        _lenS = 256 - jax.random.randint(jax.random.fold_in(_rk, 7), (8,), 0, max(1, 256 // 4) + 1, jnp.int32)
        _lenS2 = 1601 - jax.random.randint(jax.random.fold_in(_rk, 8), (8,), 0, max(1, 1601 // 4) + 1, jnp.int32)
        _ctx_512P = jax.random.normal(jax.random.fold_in(_rk, 11), (8, 16, 64), jnp.float32)
        _ctx_512c = jax.random.dirichlet(jax.random.fold_in(_rk, 511), 0.3 * jnp.ones((16,), jnp.float32), (8, 1601))
        _ctx_512t = jnp.einsum('bsk,bkd->bsd', _ctx_512c, _ctx_512P)
        _ctx_512t = _ctx_512t * jax.lax.rsqrt(jnp.mean(jnp.square(_ctx_512t)) + 1e-12) * 0.953939
        ctx_512 = 4.13588e-05 + 0.999923 * (_ctx_512t + 0.3 * jax.random.normal(jax.random.fold_in(_rk, 611), (8, 1601, 64), jnp.float32))
        return (x, ctx_512)
    x, ctx_512 = _rec_inputs()

    def _L0_xattn_setup():
        import jax, jax.numpy as jnp
        import numpy as np
        B, LQ, LK = (8, 256, 256)
        QD, KD, VD = (128, 64, 64)
        key = jax.random.key(seed)
        ks = jax.random.split(key, 9)
        s = 0.02
        return {'query': jax.random.normal(ks[0], (B, LQ, QD), jnp.float32), 'key': jax.random.normal(ks[1], (B, LK, KD), jnp.float32), 'value': jax.random.normal(ks[2], (B, LK, VD), jnp.float32), 'Wq': jax.random.normal(ks[3], (QD, QD), jnp.float32) * s, 'bq': jnp.zeros((QD,), jnp.float32), 'Wk': jax.random.normal(ks[4], (KD, QD), jnp.float32) * s, 'bk': jnp.zeros((QD,), jnp.float32), 'Wv': jax.random.normal(ks[5], (VD, QD), jnp.float32) * s, 'bv': jnp.zeros((QD,), jnp.float32)}
    _L0_xattn_all = _L0_xattn_setup()
    _L0_xattn_in = {k: v for k, v in _L0_xattn_all.items() if k in ('Wq', 'bq', 'Wk', 'bk', 'Wv', 'bv')}
    del _L0_xattn_all

    def _L0_ffn_setup():
        import jax, jax.numpy as jnp
        import numpy as np
        D, H, O, E, TOPK = (128, 512, 128, 8, 2)
        B, S = (4, 128)
        key = jax.random.key(seed)
        ks = jax.random.split(key, 12)
        std = 0.02
        return {'hidden_states': jax.random.normal(ks[0], (B, S, D), dtype=jnp.float32), 'norm_weight': jnp.ones((D,), dtype=jnp.float32), 'router_w': jax.random.normal(ks[1], (E, D), dtype=jnp.float32) * std, 'sw1': jax.random.normal(ks[2], (D, H), dtype=jnp.float32) * (1.0 / np.sqrt(D)), 'sb1': jnp.zeros((H,), dtype=jnp.float32), 'sw2': jax.random.normal(ks[3], (H, O), dtype=jnp.float32) * (1.0 / np.sqrt(H)), 'sb2': jnp.zeros((O,), dtype=jnp.float32), 'ew1': jax.random.normal(ks[4], (E, D, H), dtype=jnp.float32) * (1.0 / np.sqrt(D)), 'eb1': jnp.zeros((E, H), dtype=jnp.float32), 'ew2': jax.random.normal(ks[5], (E, H, O), dtype=jnp.float32) * (1.0 / np.sqrt(H)), 'eb2': jnp.zeros((E, O), dtype=jnp.float32)}
    _L0_ffn_all = _L0_ffn_setup()
    _L0_ffn_in = {k: v for k, v in _L0_ffn_all.items() if k in ('norm_weight', 'router_w', 'sw1', 'sb1', 'sw2', 'sb2', 'ew1', 'eb1', 'ew2', 'eb2')}
    del _L0_ffn_all
    return {'x': x, 'ctx_512': ctx_512, 'L0_xattn_Wq': _L0_xattn_in['Wq'], 'L0_xattn_bq': _L0_xattn_in['bq'], 'L0_xattn_Wk': _L0_xattn_in['Wk'], 'L0_xattn_bk': _L0_xattn_in['bk'], 'L0_xattn_Wv': _L0_xattn_in['Wv'], 'L0_xattn_bv': _L0_xattn_in['bv'], 'L0_ffn_norm_weight': _L0_ffn_in['norm_weight'], 'L0_ffn_router_w': _L0_ffn_in['router_w'], 'L0_ffn_sw1': _L0_ffn_in['sw1'], 'L0_ffn_sb1': _L0_ffn_in['sb1'], 'L0_ffn_sw2': _L0_ffn_in['sw2'], 'L0_ffn_sb2': _L0_ffn_in['sb2'], 'L0_ffn_ew1': _L0_ffn_in['ew1'], 'L0_ffn_eb1': _L0_ffn_in['eb1'], 'L0_ffn_ew2': _L0_ffn_in['ew2'], 'L0_ffn_eb2': _L0_ffn_in['eb2']}

def reference(x, ctx_512, L0_xattn_Wq, L0_xattn_bq, L0_xattn_Wk, L0_xattn_bk, L0_xattn_Wv, L0_xattn_bv, L0_ffn_norm_weight, L0_ffn_router_w, L0_ffn_sw1, L0_ffn_sb1, L0_ffn_sw2, L0_ffn_sb2, L0_ffn_ew1, L0_ffn_eb1, L0_ffn_ew2, L0_ffn_eb2):
    import jax
    import jax.numpy as jnp

    def _L0_xattn_ref(query, key, value, Wq, bq, Wk, bk, Wv, bv):
        import jax, jax.numpy as jnp
        import numpy as np
        B, LQ, LK = (8, 256, 256)
        QD, KD, VD = (128, 64, 64)
        q = jnp.einsum('bld,de->ble', query, Wq) + bq
        k = jnp.einsum('bld,de->ble', key, Wk) + bk
        v = jnp.einsum('bld,de->ble', value, Wv) + bv
        scores = jnp.einsum('bqe,bke->bqk', q, k)
        attn = jax.nn.softmax(scores, axis=-1)
        out = jnp.einsum('bqk,bke->bqe', attn, v)
        return out

    def _L0_ffn_ref(hidden_states, norm_weight, router_w, sw1, sb1, sw2, sb2, ew1, eb1, ew2, eb2):
        import jax, jax.numpy as jnp
        import numpy as np
        D, H, O, E, TOPK = (128, 512, 128, 8, 2)
        B, S = (4, 128)
        b, s, d = hidden_states.shape
        var = jnp.mean(jnp.square(hidden_states), axis=-1, keepdims=True)
        normed = hidden_states * jax.lax.rsqrt(var + 1e-08) * norm_weight
        shared = jnp.maximum(normed @ sw1 + sb1, 0.0) @ sw2 + sb2
        flat = normed.reshape(-1, d)
        T = flat.shape[0]
        probs = jax.nn.sigmoid(flat @ router_w.T)
        scores, idx = jax.lax.top_k(probs, TOPK)
        w = scores / (jnp.sum(scores, axis=-1, keepdims=True) + 1e-06)
        comb = jnp.zeros((T, E), dtype=flat.dtype)
        comb = comb.at[jnp.arange(T)[:, None], idx].add(w)
        h = jnp.maximum(jnp.einsum('td,edh->teh', flat, ew1) + eb1[None, :, :], 0.0)
        eo = jnp.einsum('teh,eho->teo', h, ew2) + eb2[None, :, :]
        routed = jnp.einsum('teo,te->to', eo, comb)
        return shared + routed.reshape(b, s, -1)
    x = x + _L0_xattn_ref(_layernorm(x, axis=-1), ctx_512, ctx_512, L0_xattn_Wq, L0_xattn_bq, L0_xattn_Wk, L0_xattn_bk, L0_xattn_Wv, L0_xattn_bv)
    x = x + _L0_ffn_ref(_layernorm(x, axis=-1), L0_ffn_norm_weight, L0_ffn_router_w, L0_ffn_sw1, L0_ffn_sb1, L0_ffn_sw2, L0_ffn_sb2, L0_ffn_ew1, L0_ffn_eb1, L0_ffn_ew2, L0_ffn_eb2)
    return x

_drawn_inputs = setup_inputs


def setup_inputs(seed=0):
    import zlib

    import numpy as np

    out = dict(_drawn_inputs(seed))
    spreads = {'L0_xattn_bq': (0.0, 0.278),
     'L0_xattn_bk': (0.0, 0.8),
     'L0_xattn_bv': (0.0, 0.1),
     'L0_ffn_norm_weight': (1.0, 0.2),
     'L0_ffn_sb1': (0.0, 0.1),
     'L0_ffn_sb2': (0.0, 0.1),
     'L0_ffn_eb1': (0.0, 0.1),
     'L0_ffn_eb2': (0.0, 0.1)}
    factors = {}
    for name, (base, spread) in spreads.items():
        noise = np.random.default_rng([zlib.crc32(name.encode()), seed]).standard_normal(out[name].shape)
        drawn = base * np.exp(spread * noise) if base else spread * noise
        out[name] = jnp.asarray(drawn.astype(out[name].dtype))
    for name, factor in factors.items():
        out[name] = (out[name] * factor).astype(out[name].dtype)
    return out
```

```python
from contextlib import ExitStack

import concourse.bass as bass
from concourse import mybir

F32 = mybir.dt.float32
F32R = mybir.dt.float32r
ALU = mybir.AluOpType
ACT = mybir.ActivationFunctionType
AX = mybir.AxisListType.X

P = 128


def wait(eng, sem, value):
    if not (isinstance(value, int) and value <= 0):
        eng.wait_ge(sem, value)


class Chain:

    def __init__(self, eng, sem):
        self.eng, self.sem, self.base, self.n = eng, sem, 0, 0

    def step(self, ins):
        ins.then_inc(self.sem, 1)
        self.n += 1
        self.eng.wait_ge(self.sem, self.base + self.n)

    def enter(self, i, per_round):
        self.first, self.per_round = self.n, per_round
        self.base = (i - 1) * per_round

    def leave(self, rounds):
        assert self.n == self.first + self.per_round, (self.n - self.first, self.per_round)
        self.base, self.n = 0, self.first + rounds * self.per_round


def xattn_moe_kernel(nc, x, ctx, Wq, bq, Wk, bk, Wv, bv, nw, router_w, sw1, sb1, sw2, sb2,
                     ew1, eb1, ew2, eb2, out):
    B, LQ, D = x.shape
    NK, KD = ctx.shape[1:]
    E, _, H = ew1.shape
    T = B * LQ
    NT = T // P
    HB = H // P
    KT = NK // P
    TAIL = NK - KT * P
    TAILE = TAIL + TAIL % 2
    NKT = KT + 1
    NE = E + 1
    CH = 512
    NC = T // CH
    BLK = NE * HB
    PAIRS = B // 2
    assert D == P and LQ == 2 * P and 2 * KD == P and T % CH == 0 and B % 2 == 0

    GROUPS = [(a, min(a + 4, NKT)) for a in range(0, NKT, 4)]
    NG = len(GROUPS)

    def tile_rows(j):
        return P if j < KT else TAIL

    xt = x.rearrange("b (s p) d -> p (b s) d", p=P)
    ot = out.rearrange("b (s p) d -> p (b s) d", p=P)
    comb_d = nc.dram_tensor("comb_scratch", (E, T), F32, kind="Internal").ap()

    with ExitStack() as st:
        def sb(name, shape, dt=F32, ctx_=None):
            return (ctx_ or st).enter_context(nc.sbuf_tensor(name, shape, dt))

        def sem(name):
            return st.enter_context(nc.semaphore(name))

        xa = sb("xa", [P, NT, D])
        xTh = sb("xTh", [P, T], F32R)
        xTl = sb("xTl", [P, T], F32R)
        Wh = sb("Wh", [P, NE, 2 * H], F32R)
        Wl = sb("Wl", [P, NE, 2 * H], F32R)
        ident = sb("ident", [P, P])
        cols = sb("cols", [P, BLK + 4])
        B1, BQ, BK, NW, SB2 = 0, BLK, BLK + 1, BLK + 2, BLK + 3
        eb2s = sb("eb2s", [E, D])
        lgT = sb("lgT", [E, T])
        combT = sb("combT", [E, T])
        rwTh = sb("rwTh", [P, E], F32R)
        rwTl = sb("rwTl", [P, E], F32R)

        ph1 = ExitStack()
        craw = [sb(f"craw{u}", [P, NKT, KD], F32, ph1) for u in range(2)]
        cnat = [sb(f"cnat{u}", [P, NKT, 2 * KD], F32R, ph1) for u in range(2)]
        cT = [sb(f"cT{u}", [P, KT * P + TAILE], F32R, ph1) for u in range(2)]
        probs = [sb(f"probs{s}", [P, NK + NK % 2], F32, ph1) for s in range(2)]
        pTh = sb("pTh", [P, NKT, P], F32R, ph1)
        pTl = sb("pTl", [P, NKT, P], F32R, ph1)
        wraw = [sb(f"wraw{u}", [P, 2 * H], F32, ph1) for u in range(2)]
        xn = sb("xn", [P, 2, D], F32, ph1)
        yn = sb("yn", [P, 2, D], F32, ph1)
        xnT = sb("xnT", [P, LQ], F32, ph1)
        qh = sb("qh", [P, LQ], F32R, ph1)
        ql = sb("ql", [P, LQ], F32R, ph1)
        oT = sb("oT", [P, P], F32, ph1)
        st6 = [sb(f"st6{i}", [P, 2, 6], F32, ph1) for i in range(2)]
        mv1 = [sb(f"mv1{u}", [P, 2, 2], F32, ph1) for u in range(2)]
        mv2 = sb("mv2", [P, 2, 2], F32, ph1)
        lnt = sb("lnt", [P, 8, 2], F32, ph1)
        mhalf = sb("mhalf", [P, 2], F32, ph1)
        eps1 = sb("eps1", [P, 2], F32, ph1)
        eps2 = sb("eps2", [P, 2], F32, ph1)
        zero = sb("zero", [P, 1], F32, ph1)
        mx = sb("mx", [P, 4], F32, ph1)
        nbias = [sb(f"nbias{s}", [P, 1], F32, ph1) for s in range(2)]
        rsum = [sb(f"rsum{s}", [P, 2], F32, ph1) for s in range(2)]
        rinv = sb("rinv", [P, 2], F32, ph1)
        cq = [sb(f"cq{u}", [P, 2], F32, ph1) for u in range(2)]
        rows = sb("rows", [BLK + 4, P], F32, ph1)
        wq_s = sb("wq_s", [P, D], F32, ph1)
        wk_s = sb("wk_s", [KD, D], F32, ph1)
        wv2 = sb("wv2", [P, D], F32, ph1)
        rw_s = sb("rw_s", [E, D], F32, ph1)
        bvB = sb("bvB", [P, D], F32, ph1)
        wqT = sb("wqT", [P, D], F32, ph1)
        wk2T = sb("wk2T", [P, 2 * KD + 1], F32, ph1)
        wqk = sb("wqk", [P, 2 * KD + 1], F32, ph1)
        rwT = sb("rwT", [P, E], F32, ph1)
        bqk = sb("bqk", [P, 2], F32, ph1)
        bqrep = sb("bqrep", [P, P], F32, ph1)
        ph1.close()
        comb = sb("comb", [P, NT, E])
        ph2 = ExitStack()
        lowi = sb("lowi", [P, E, E], F32, ph2)
        pr = sb("pr", [P, NT, E], F32, ph2)
        rk = [sb(f"rk{i}", [P, NT, E, E], F32, ph2) for i in range(2)]
        rank = sb("rank", [P, NT, E], F32, ph2)
        den = sb("den", [P, NT], F32, ph2)
        ph2.close()
        cb = sb("cb", [P, E, T])
        rl = [sb(f"rl{i}", [P, CH]) for i in range(2)]
        hh = [sb(f"hh{j}", [P, CH], F32R) for j in range(HB)]
        hl = [sb(f"hl{j}", [P, CH], F32R) for j in range(HB)]
        acc = sb("acc", [P, CH])
        tmp = [sb(f"tmp{i}", [P, CH]) for i in range(2)]
        fin = sb("fin", [P, CH])
        outs = sb("outs", [P, CH // P, D])

        ps = st.enter_context(nc.psum_tensor("ps", [P, 8, 512], F32))
        S = ps[:, 0:4, :].rearrange("p a b -> p (a b)")
        PT = [ps[:, 4, :], ps[:, 5, :]]
        PV = ps[:, 6, 0:P]
        MI = ps[:, 7, :]

        x_in0, x_in1, setup_in = sem("x_in0"), sem("x_in1"), sem("setup_in")
        ctx_in = [sem("ctx_in0"), sem("ctx_in1")]
        w_in = [sem("w_in0"), sem("w_in1")]
        consts = sem("consts")
        setT, setT_out = sem("setT"), sem("setT_out")
        setM, setM_out = sem("setM"), sem("setM_out")
        c_split = sem("c_split")
        w_split = sem("w_split")
        pool_chain, dve_chain = sem("pool_chain"), sem("dve_chain")
        stats1, stats2 = sem("stats1"), sem("stats2")
        ln1, ln2 = sem("ln1"), sem("ln2")
        cT_full, cT_out = sem("cT_full"), sem("cT_out")
        xnT_full, xnT_out = sem("xnT_full"), sem("xnT_out")
        q_full, qh_out, q_out = sem("q_full"), sem("qh_out"), sem("q_out")
        s_done = sem("s_done")
        bias_done = sem("bias_done")
        exp_done = sem("exp_done")
        pt_full, pth_out, ptl_out = sem("pt_full"), sem("pth_out"), sem("ptl_out")
        pv_done, oT_out = sem("pv_done"), sem("oT_out")
        o_done, x1_out = sem("o_done"), sem("x1_out")
        yT_full, yTh_out, yT_out = sem("yT_full"), sem("yTh_out"), sem("yT_out")
        lg_full = sem("lg_full")
        lgT_full, lgT_out = sem("lgT_full"), sem("lgT_out")
        xb_out, bqk_out = sem("xb_out"), sem("bqk_out")
        nexp, comb_done, combT_full, combT_out = sem("nexp"), sem("comb_done"), sem("combT_full"), sem("combT_out")
        comb_st, cb_in0, cb_in1 = sem("comb_st"), sem("cb_in0"), sem("cb_in1")
        up_done, relu_out, hh_out, split_out = sem("up_done"), sem("relu_out"), sem("hh_out"), sem("split_out")
        down_done = sem("down_done")
        acc_first, tmp_out, acc_out = sem("acc_first"), sem("tmp_out"), sem("acc_out")
        fin_out, finT_full, outs_out, out_st = sem("fin_out"), sem("finT_full"), sem("outs_out"), sem("out_st")
        low_done = sem("low_done")

        block = st.enter_context(nc.Block())

        @block.sync
        def _(sp):
            def load_ctx(b, u):
                nc.sync.dma_start(craw[u][:, 0:KT, :], ctx[b, 0:KT * P, :].rearrange("(p j) d -> p j d", j=KT)).then_inc(ctx_in[u], 16)
                nc.sync.dma_start(craw[u][0:TAIL, KT, :], ctx[b, KT * P:NK, :]).then_inc(ctx_in[u], 16)

            def load_weights(w1, w2, u):
                nc.sync.dma_start(wraw[u][:, 0:H], w1).then_inc(w_in[u], 16)
                nc.sync.dma_start(wraw[u][:, H:2 * H].rearrange("p (j o) -> p j o", j=HB),
                                  w2.rearrange("(j p) o -> p j o", p=P)).then_inc(w_in[u], 16)

            nc.sync.dma_start(xa[:, 0:4, :], xt[:, 0:4, :]).then_inc(x_in0, 16)
            nc.sync.dma_start(wq_s[:], Wq).then_inc(setup_in, 16)
            nc.sync.dma_start(wk_s[:], Wk).then_inc(setup_in, 16)
            nc.sync.dma_start(rows[0:E * HB, :], eb1.rearrange("e (j p) -> (e j) p", p=P)).then_inc(setup_in, 16)
            nc.sync.dma_start(rows[E * HB:BLK, :], sb1.rearrange("(j p) -> j p", p=P)).then_inc(setup_in, 16)
            for r, v in ((BQ, bq), (BK, bk), (NW, nw), (SB2, sb2)):
                nc.sync.dma_start(rows[r:r + 1, :], v.rearrange("(a p) -> a p", a=1)).then_inc(setup_in, 16)
            nc.sync.dma_start(rw_s[:], router_w).then_inc(setup_in, 16)
            nc.sync.dma_start(wv2[0:KD, :], Wv).then_inc(setup_in, 16)
            nc.sync.dma_start(wv2[KD:P, :], Wv).then_inc(setup_in, 16)
            nc.sync.dma_start(bvB[:], bv.partition_broadcast(P)).then_inc(setup_in, 16)
            nc.sync.dma_start(eb2s[:], eb2).then_inc(setup_in, 16)
            sp.wait_ge(consts, 1)
            load_ctx(0, 0)
            load_ctx(1, 1)
            nc.sync.dma_start(xa[:, 4:NT, :], xt[:, 4:NT, :]).then_inc(x_in1, 16)
            load_weights(sw1, sw2, 0)
            load_weights(ew1[0], ew2[0], 1)

            def batch(b, u, last):
                if not last:
                    wait(sp, c_split, b + 1)
                    load_ctx(b + 2, u)
                if not (last and u == 1):
                    wait(sp, w_split, b + 1)
                    load_weights(ew1[b + 1], ew2[b + 1], u)

            batch(0, 0, False)
            batch(1, 1, False)
            with sp.Fori(1, PAIRS - 1) as i:
                batch(2 * i, 0, False)
                batch(2 * i + 1, 1, False)
            batch(B - 2, 0, True)
            batch(B - 1, 1, True)

            sp.wait_ge(combT_out, 1)
            nc.sync.dma_start(comb_d, combT[:]).then_inc(comb_st, 16)
            sp.wait_ge(comb_st, 16)
            sp.wait_ge(w_split, NE)
            nc.sync.dma_start(cb[:, :, 0:CH], comb_d[:, 0:CH].partition_broadcast(P)).then_inc(cb_in0, 16)
            for c in range(1, NC):
                nc.sync.dma_start(cb[:, :, c * CH:(c + 1) * CH],
                                  comb_d[:, c * CH:(c + 1) * CH].partition_broadcast(P)).then_inc(cb_in1, 16)
            with sp.Fori(0, NC) as c:
                sp.wait_ge(outs_out, c + 1)
                nc.sync.dma_start(ot[:, bass.ts(c, CH // P), :], outs[:]).then_inc(out_st, 16)
            sp.wait_ge(out_st, 16 * NC)

        @block.gpsimd
        def _(pool):
            ch = Chain(pool, pool_chain)
            gp = nc.gpsimd

            gp.memset(craw[0][:, KT, :], 0.0)
            gp.memset(craw[1][:, KT, :], 0.0).then_inc(consts, 1)
            ch.step(gp.memset(ident[:], 0.0))
            gp.affine_select(out=ident[:], in_=ident[:], compare_op=ALU.not_equal, fill=1.0, base=0,
                             pattern=[[-1, P]], channel_multiplier=1).then_inc(consts, 1)
            gp.memset(eps1[:], 1e-5)
            gp.memset(eps2[:], 1e-8)
            gp.memset(zero[:], 0.0)
            ch.step(gp.memset(mhalf[:], -0.5))

            def split_ctx(b, k, first=False):
                wait(pool, ctx_in[k], (b + (2 - k)) * 16)
                if not first:
                    wait(pool, pv_done, NG * 2 * (b - 1))
                ch.step(gp.tensor_tensor(cnat[k][:, :, 0:KD], craw[k][:],
                                         zero[:].unsqueeze(2).broadcast_to([P, NKT, KD]), ALU.add))
                gp.tensor_tensor(cnat[k][:, :, KD:2 * KD], craw[k][:], cnat[k][:, :, 0:KD].bitcast(F32),
                                 ALU.subtract).then_inc(c_split, 1)

            def split_weights(e, n, u):
                wait(pool, w_in[u], (n + (2 - u)) * 16)
                ch.step(gp.tensor_tensor(Wh[:, e, :], wraw[u][:], zero[:].broadcast_to([P, 2 * H]), ALU.add))
                gp.tensor_tensor(Wl[:, e, :], wraw[u][:], Wh[:, e, :].bitcast(F32), ALU.subtract).then_inc(w_split, 1)

            def norm1(b, k, first=False):
                pool.wait_ge(stats1, b + 1)
                if not first:
                    pool.wait_ge(xnT_full, b)
                gp.tensor_tensor(lnt[:, 0, :], mv1[k][:, :, 1], eps1[:], ALU.add)
                ch.step(gp.tensor_tensor(xn[:], xa[:, bass.ts(b, 2), :],
                                         mv1[k][:, :, 0].unsqueeze(2).broadcast_to([P, 2, D]), ALU.subtract))
                ch.step(gp.tensor_tensor(lnt[:, 1, :], lnt[:, 0, :], mhalf[:], ALU.pow))
                gp.tensor_tensor(xn[:], xn[:], lnt[:, 1, :].unsqueeze(2).broadcast_to([P, 2, D]),
                                 ALU.mult).then_inc(ln1, 1)
                gp.tensor_tensor(xa[:, bass.ts(b, 2), :], xa[:, bass.ts(b, 2), :],
                                 bvB[:].unsqueeze(1).broadcast_to([P, 2, D]), ALU.add).then_inc(xb_out, 1)

            def norm2(b, k):
                pool.wait_ge(stats2, b + 1)
                if not (isinstance(b, int) and b == 0):
                    pool.wait_ge(yT_full, b)
                gp.tensor_tensor(lnt[:, 2, :], mv2[:, :, 1], eps1[:], ALU.add)
                ch.step(gp.tensor_tensor(yn[:], xa[:, bass.ts(b, 2), :],
                                         mv2[:, :, 0].unsqueeze(2).broadcast_to([P, 2, D]), ALU.subtract))
                ch.step(gp.tensor_tensor(lnt[:, 3, :], lnt[:, 2, :], mhalf[:], ALU.pow))
                ch.step(gp.tensor_tensor(lnt[:, 4, :], mv2[:, :, 1], lnt[:, 3, :], ALU.mult))
                ch.step(gp.tensor_tensor(lnt[:, 5, :], lnt[:, 4, :], lnt[:, 3, :], ALU.mult))
                ch.step(gp.tensor_tensor(lnt[:, 6, :], lnt[:, 5, :], eps2[:], ALU.add))
                ch.step(gp.tensor_tensor(lnt[:, 7, :], lnt[:, 6, :], mhalf[:], ALU.pow))
                ch.step(gp.tensor_tensor(lnt[:, 0, :], lnt[:, 7, :], lnt[:, 3, :], ALU.mult))
                gp.tensor_tensor(yn[:], yn[:], lnt[:, 0, :].unsqueeze(2).broadcast_to([P, 2, D]),
                                 ALU.mult).then_inc(ln2, 1)

            split_ctx(0, 0, first=True)
            pool.wait_ge(setup_in, 16 * 13)
            norm1(0, 0, first=True)

            def batch(b, k, last=False):
                if not last:
                    split_ctx(b + 1, 1 - k, first=isinstance(b, int) and b == 0)
                    norm1(b + 1, 1 - k)
                if not (isinstance(b, int) and b == 0):
                    norm2(b - 1, 1 - k)
                if isinstance(b, int) and b == 0:
                    split_weights(E, 0, 0)
                split_weights(b, b + 1, 1 - k)

            batch(0, 0)
            batch(1, 1)
            with pool.Fori(1, PAIRS - 1) as i:
                ch.enter(i, 2 * (1 + 2 + 7 + 1))
                batch(2 * i, 0)
                batch(2 * i + 1, 1)
            ch.leave(PAIRS - 2)
            batch(B - 2, 0)
            batch(B - 1, 1, last=True)
            norm2(B - 1, 1)
            pool.wait_ge(yT_full, B)
            ch.step(gp.memset(lowi[:], 1.0))
            gp.affine_select(out=lowi[:], in_=lowi[:], compare_op=ALU.is_gt, fill=0.0, base=0,
                             pattern=[[1, E], [-1, E]], channel_multiplier=0).then_inc(low_done, 1)

            def sums(c):
                for e in range(1, E):
                    pool.wait_ge(tmp_out, (E - 1) * c + e)
                    if e == 1:
                        pool.wait_ge(acc_first, c + 1)
                    gp.tensor_tensor(acc[:], acc[:], tmp[e % 2][:], ALU.add).then_inc(acc_out, 1)
                    pool.wait_ge(acc_out, (E - 1) * c + e)
            with pool.Fori(0, NC) as c:
                sums(c)

        @block.scalar
        def _(act):
            a = nc.scalar

            act.wait_ge(setT, 4)
            a.copy(wqT[:], ps[:, 0, 0:D]).then_inc(setT_out, 1)
            a.copy(cols[:], ps[:, 2, 0:BLK + 4]).then_inc(setT_out, 1)
            a.copy(rwT[:], ps[:, 3, 0:E]).then_inc(setT_out, 1)
            act.wait_ge(setM, 3)
            a.copy(wqk[:], ps[:, 0, 0:2 * KD + 1]).then_inc(setM_out, 1)

            def ctx_groups(b, k):
                for g, (j0, j1) in enumerate(GROUPS):
                    act.wait_ge(cT_full, NG * b + g + 1)
                    w = (j1 - j0) * P if j1 <= KT else TAILE
                    a.copy(cT[k][:, j0 * P:j0 * P + w], PT[g % 2][:, 0:w]).then_inc(cT_out, 1)

            def queries(b):
                act.wait_ge(xnT_full, b + 1)
                a.copy(xnT[:], MI[:, 0:LQ]).then_inc(xnT_out, 1)
                act.wait_ge(q_full, b + 1)
                a.activation(qh[:], MI[:, 0:LQ], ACT.Identity, bias=bqk[:, 0:1]).then_inc(qh_out, 1)

            def exps(g, s):
                act.wait_ge(bias_done, g + 1)
                a.activation(probs[s][:, 0:1024], S[:, 0:1024], ACT.Exp, bias=nbias[s][:],
                             accum_out=rsum[s][:, 0:1]).then_inc(exp_done, 1)
                a.activation(probs[s][:, 1024:NK], S[:, 1024:NK], ACT.Exp, bias=nbias[s][:],
                             accum_out=rsum[s][:, 1:2]).then_inc(exp_done, 1)

            def prob_groups(g):
                for n, (j0, j1) in enumerate(GROUPS):
                    act.wait_ge(pt_full, NG * g + n + 1)
                    r = tile_rows(j1 - 1)
                    a.copy(pTh[0:r, j0:j1, :].rearrange("p a b -> p (a b)"),
                           PT[n % 2][0:r, 0:(j1 - j0) * P]).then_inc(pth_out, 1)

            def attn_out(g):
                act.wait_ge(pv_done, NG * (g + 1))
                a.copy(oT[:], PV).then_inc(oT_out, 1)

            def normedT(b):
                act.wait_ge(yT_full, b + 1)
                a.activation(xTh[:, bass.ts(b, LQ)], MI[:, 0:LQ], ACT.Copy, scale=cols[:, NW:NW + 1]).then_inc(yTh_out, 1)

            ctx_groups(0, 0)
            act.wait_ge(bqk_out, 1)
            queries(0)

            def batch(b, k, last=False):
                for s in range(2):
                    g = 2 * b + s
                    exps(g, s)
                    prob_groups(g)
                    attn_out(g)
                    if s == 0 and not last:
                        ctx_groups(b + 1, 1 - k)
                        queries(b + 1)
                    if s == 1 and not (isinstance(b, int) and b == 0):
                        normedT(b - 1)

            batch(0, 0)
            batch(1, 1)
            with act.Fori(1, PAIRS - 1) as i:
                batch(2 * i, 0)
                batch(2 * i + 1, 1)
            batch(B - 2, 0)
            batch(B - 1, 1, last=True)
            normedT(B - 1)

            act.wait_ge(lg_full, 1)
            a.activation(pr[:].rearrange("p t e -> p (t e)"), MI[:, 0:NT * E], ACT.Exp, scale=-1.0).then_inc(nexp, 1)
            act.wait_ge(combT_full, 1)
            a.copy(combT[:], S[0:E, 0:T]).then_inc(combT_out, 1)

            def relus(c):
                for m in range(BLK):
                    j = m % HB
                    act.wait_ge(up_done, BLK * c + m + 1)
                    wait(act, split_out, BLK * c + m - 1)
                    a.activation(rl[m % 2][:], ps[:, j, :], ACT.Relu, bias=cols[:, B1 + m:B1 + m + 1]).then_inc(relu_out, 1)
            relus(0)
            with act.Fori(1, NC) as c:
                relus(c)

        @block.tensor
        def _(pe):
            mm, tr = nc.tensor.matmul, nc.tensor.transpose

            pe.wait_ge(consts, 2)
            pe.wait_ge(setup_in, 16 * 13)
            tr(ps[:, 0, 0:D], wq_s[:], ident[:]).then_inc(setT, 1)
            tr(ps[:, 1, 0:KD], wk_s[:], ident[0:KD, 0:KD]).then_inc(setT, 1)
            tr(ps[:, 2, 0:BLK + 4], rows[:], ident[0:BLK + 4, 0:BLK + 4]).then_inc(setT, 1)
            tr(ps[:, 3, 0:E], rw_s[:], ident[0:E, 0:E]).then_inc(setT, 1)
            pe.wait_ge(setT_out, 6)
            mm(ps[:, 0, 0:2 * KD + 1], wqT[:], wk2T[:], start=True, stop=True).then_inc(setM, 1)
            mm(ps[:, 1, 0:1], wk2T[:, 0:2 * KD], cols[:, BQ:BQ + 1], start=True, stop=True).then_inc(setM, 1)
            mm(ps[:, 2, 0:1], bqrep[:], cols[:, BK:BK + 1], start=True, stop=True).then_inc(setM, 1)

            def ctx_groups(b, k):
                pe.wait_ge(c_split, b + 1)
                for g, (j0, j1) in enumerate(GROUPS):
                    if g < 2:
                        wait(pe, ptl_out, NG * (2 * b - 1) - 1 + g)
                    else:
                        pe.wait_ge(cT_out, NG * b + g - 1)
                    for j in range(j0, j1):
                        r = P if j < KT else TAILE
                        last = tr(PT[g % 2][:, (j - j0) * P:(j - j0) * P + r],
                                  cnat[k][0:r, j, :].bitcast(F32), ident[0:r, 0:r])
                    last.then_inc(cT_full, 1)

            def queries(b):
                pe.wait_ge(ln1, b + 1)
                wait(pe, x1_out, 2 * b - 1)
                for s in range(2):
                    last = tr(MI[:, s * P:(s + 1) * P], xn[:, s, :], ident[:])
                last.then_inc(xnT_full, 1)
                pe.wait_ge(xnT_out, b + 1)
                mm(MI[:, 0:LQ], wqk[:, 0:2 * KD], xnT[:], start=True, stop=True)
                for s in range(2):
                    last = mm(MI[:, LQ + s:LQ + s + 1], xnT[:, s * P:(s + 1) * P], wqk[:, 2 * KD:2 * KD + 1],
                              start=True, stop=True)
                last.then_inc(q_full, 1)

            def scores(g, b, k, s):
                if s == 0:
                    pe.wait_ge(cT_out, NG * (b + 1))
                    pe.wait_ge(q_out, b + 1)
                for half in range(2):
                    wait(pe, exp_done, 2 * g - 1 + half)
                    for a0 in range(1024 * half, min(1024 * half + 1024, KT * P + TAILE), 512):
                        w = min(512, KT * P + TAILE - a0)
                        mm(S[:, a0:a0 + w], qh[:, s * P:(s + 1) * P], cT[k][:, a0:a0 + w], start=True, stop=False)
                        last = mm(S[:, a0:a0 + w], ql[:, s * P:(s + 1) * P], cT[k][:, a0:a0 + w], start=False, stop=True)
                    last.then_inc(s_done, 1)

            def attend(g, k, s, after_ctx):
                def turn(n):
                    j0, j1 = GROUPS[n]
                    if n >= 2 or not after_ctx:
                        pe.wait_ge(ptl_out, NG * g + n - 1)
                    for j in range(j0, j1):
                        r = tile_rows(j)
                        last = tr(PT[n % 2][0:r, (j - j0) * P:(j - j0 + 1) * P],
                                  probs[s][:, j * P:j * P + r], ident[:])
                    last.then_inc(pt_full, 1)

                def product(n):
                    j0, j1 = GROUPS[n]
                    pe.wait_ge(ptl_out, NG * g + n + 1)
                    if n == 0:
                        wait(pe, oT_out, g)
                    for j in range(j0, j1):
                        r = tile_rows(j)
                        mm(PV, cnat[k][0:r, j, :], pTh[0:r, j, :], start=(j == 0), stop=False)
                        last = mm(PV, cnat[k][0:r, j, :], pTl[0:r, j, :], start=False, stop=(j == NKT - 1))
                    last.then_inc(pv_done, 1)

                pe.wait_ge(exp_done, 2 * g + 2)
                turn(0)
                turn(1)
                for n in range(NG):
                    product(n)
                    if n + 2 < NG:
                        turn(n + 2)

            def project(g, b, s):
                pe.wait_ge(oT_out, g + 1)
                wait(pe, x1_out, g)
                if s == 0:
                    wait(pe, lgT_out, b - 1)
                mm(MI[:, 0:D], oT[:], wv2[:], start=True, stop=True).then_inc(o_done, 1)

            def normedT(b, g):
                pe.wait_ge(ln2, b + 1)
                pe.wait_ge(x1_out, g + 1)
                for s in range(2):
                    last = tr(MI[:, s * P:(s + 1) * P], yn[:, s, :], ident[:])
                last.then_inc(yT_full, 1)

            def router(b):
                pe.wait_ge(yT_out, b + 1)
                t = bass.ts(b, LQ)
                mm(MI[0:E, 0:LQ], rwTh[:], xTh[:, t], start=True, stop=False)
                mm(MI[0:E, 0:LQ], rwTh[:], xTl[:, t], start=False, stop=False)
                mm(MI[0:E, 0:LQ], rwTl[:], xTh[:, t], start=False, stop=True).then_inc(lgT_full, 1)

            ctx_groups(0, 0)
            pe.wait_ge(setM_out, 1)
            pe.wait_ge(bqk_out, 1)
            queries(0)
            scores(0, 0, 0, 0)

            def batch(b, k, last=False):
                scores(2 * b + 1, b, k, 1)
                attend(2 * b, k, 0, after_ctx=isinstance(b, int) and b == 0)
                project(2 * b, b, 0)
                if not last:
                    ctx_groups(b + 1, 1 - k)
                    queries(b + 1)
                    scores(2 * b + 2, b + 1, 1 - k, 0)
                attend(2 * b + 1, k, 1, after_ctx=not last)
                project(2 * b + 1, b, 1)
                if not (isinstance(b, int) and b == 0):
                    normedT(b - 1, 2 * b + 1)
                    router(b - 1)

            batch(0, 0)
            batch(1, 1)
            with pe.Fori(1, PAIRS - 1) as i:
                batch(2 * i, 0)
                batch(2 * i + 1, 1)
            batch(B - 2, 0)
            batch(B - 1, 1, last=True)
            pe.wait_ge(lgT_out, B - 1)
            normedT(B - 1, 2 * B - 1)
            router(B - 1)
            pe.wait_ge(lgT_out, B)
            for t in range(NT):
                last = tr(MI[:, t * E:(t + 1) * E], lgT[:, t * P:(t + 1) * P], ident[0:E, 0:E])
            last.then_inc(lg_full, 1)

            pe.wait_ge(comb_done, 1)
            for t in range(NT):
                last = tr(S[0:E, t * P:(t + 1) * P], comb[:, t, :], ident[:])
            last.then_inc(combT_full, 1)
            pe.wait_ge(combT_out, 1)

            LAG = 3

            def up(c, m):
                e, j = m // HB, m % HB
                wait(pe, relu_out, BLK * c + m - 3)
                w = slice(j * P, (j + 1) * P)
                xs = bass.ts(c, CH)
                mm(ps[:, j, :], Wh[:, e, w], xTh[:, xs], start=True, stop=False)
                mm(ps[:, j, :], Wh[:, e, w], xTl[:, xs], start=False, stop=False)
                mm(ps[:, j, :], Wl[:, e, w], xTh[:, xs], start=False, stop=True).then_inc(up_done, 1)

            def down(c, m):
                e, j = m // HB, m % HB
                y = ps[:, 4 + e % 3, :]
                first = j == 0
                if first and e == 3:
                    pe.wait_ge(acc_first, c + 1)
                elif first and e > 3:
                    pe.wait_ge(tmp_out, (E - 1) * c + e - 3)
                elif first and e == E % 3:
                    wait(pe, fin_out, c)
                elif first:
                    wait(pe, tmp_out, (E - 1) * (c - 1) + e + 6)
                if first and e == E:
                    xs = bass.ts(c, CH)
                    mm(y, eb2s[:], combT[:, xs], start=True, stop=False)
                    first = False
                pe.wait_ge(split_out, BLK * c + m + 1)
                w = slice(H + j * P, H + (j + 1) * P)
                mm(y, Wh[:, e, w], hh[j][:], start=first, stop=False)
                mm(y, Wl[:, e, w], hh[j][:], start=False, stop=False)
                last = mm(y, Wh[:, e, w], hl[j][:], start=False, stop=(j == HB - 1))
                last.then_inc(down_done, 1)

            def out_transposes(c):
                pe.wait_ge(fin_out, c + 1)
                wait(pe, outs_out, c)
                for t in range(CH // P):
                    last = tr(MI[:, t * P:(t + 1) * P], fin[:, t * P:(t + 1) * P], ident[:])
                last.then_inc(finT_full, 1)

            def chunk(c):
                for m in range(BLK):
                    up(c, m)
                    if m >= LAG:
                        down(c, m - LAG)
                    elif not (isinstance(c, int) and c == 0):
                        down(c - 1, BLK + m - LAG)
                    if m == 8 and not (isinstance(c, int) and c == 0):
                        out_transposes(c - 1)
            pe.wait_ge(nexp, 1)
            pe.wait_ge(w_split, NE)
            chunk(0)
            with pe.Fori(1, NC) as c:
                chunk(c)
            for m in range(BLK - LAG, BLK):
                down(NC - 1, m)
            out_transposes(NC - 1)

        @block.vector
        def _(dve):
            v = nc.vector
            ch = Chain(dve, dve_chain)

            def stats(b, of):
                for s in range(2):
                    last = v.bn_stats(st6[of][:, s, :], xa[:, 2 * b + s, :])
                return last

            def moments(dst, of, done):
                for s in range(2):
                    last = v.bn_aggr(dst[:, s, :], st6[of][:, s, :])
                last.then_inc(done, 1)

            dve.wait_ge(x_in0, 16)
            for b in range(2):
                ch.step(stats(b, 0))
                moments(mv1[b], 0, stats1)
                dve.wait_ge(stats1, b + 1)

            dve.wait_ge(setT, 4)
            v.tensor_copy(wk2T[:, 0:KD], ps[:, 1, 0:KD])
            v.tensor_copy(wk2T[:, KD:2 * KD], ps[:, 1, 0:KD]).then_inc(setT_out, 1)
            dve.wait_ge(setT_out, 4)
            v.tensor_copy(wk2T[:, 2 * KD:2 * KD + 1], cols[:, BK:BK + 1]).then_inc(setT_out, 1)
            v.tensor_copy(bqrep[:], cols[:, BQ:BQ + 1].broadcast_to([P, P])).then_inc(setT_out, 1)
            ch.step(v.tensor_copy(rwTh[:], rwT[:]))
            ch.step(v.tensor_tensor(rwTl[:], rwT[:], rwTh[:].bitcast(F32), ALU.subtract))
            dve.wait_ge(setM, 3)
            v.tensor_copy(bqk[:, 0:1], ps[:, 1, 0:1])
            v.tensor_copy(bqk[:, 1:2], ps[:, 2, 0:1]).then_inc(bqk_out, 1)
            dve.wait_ge(bqk_out, 1)

            def queries(b, k):
                dve.wait_ge(qh_out, b + 1)
                v.scalar_tensor_tensor(out=ql[:], in0=MI[:, 0:LQ], scalar=bqk[:, 0:1], in1=qh[:].bitcast(F32),
                                       op0=ALU.add, op1=ALU.subtract)
                v.tensor_scalar(cq[k][:], MI[:, LQ:LQ + 2], bqk[:, 1:2], None, ALU.add).then_inc(q_out, 1)

            def row_max(g, k, s):
                dve.wait_ge(s_done, 2 * g + 1)
                v.tensor_reduce(mx[:, 0:1], S[:, 0:1024], AX, ALU.max)
                dve.wait_ge(s_done, 2 * g + 2)
                ch.step(v.tensor_reduce(mx[:, 1:2], S[:, 1024:NK], AX, ALU.max))
                ch.step(v.scalar_tensor_tensor(out=mx[:, 2:3], in0=mx[:, 0:1], scalar=mx[:, 1:2],
                                               in1=cq[k][:, s:s + 1], op0=ALU.max, op1=ALU.add))
                v.scalar_tensor_tensor(out=nbias[s][:], in0=mx[:, 2:3], scalar=-1.0, in1=cq[k][:, s:s + 1],
                                       op0=ALU.mult, op1=ALU.add).then_inc(bias_done, 1)

            def prob_groups(g):
                for n, (j0, j1) in enumerate(GROUPS):
                    dve.wait_ge(pth_out, NG * g + n + 1)
                    r = tile_rows(j1 - 1)
                    v.tensor_tensor(pTl[0:r, j0:j1, :].rearrange("p a b -> p (a b)"), PT[n % 2][0:r, 0:(j1 - j0) * P],
                                    pTh[0:r, j0:j1, :].rearrange("p a b -> p (a b)").bitcast(F32),
                                    ALU.subtract).then_inc(ptl_out, 1)

            def x1(g, b, s):
                dve.wait_ge(exp_done, 2 * g + 2)
                ch.step(v.tensor_tensor(rinv[:, 0:1], rsum[s][:, 0:1], rsum[s][:, 1:2], ALU.add))
                ch.step(v.reciprocal(rinv[:, 1:2], rinv[:, 0:1]))
                wait(dve, xb_out, b + 1)
                dve.wait_ge(o_done, g + 1)
                v.scalar_tensor_tensor(out=xa[:, g, :], in0=MI[:, 0:D], scalar=rinv[:, 1:2], in1=xa[:, g, :],
                                       op0=ALU.mult, op1=ALU.add).then_inc(x1_out, 1)

            def normedT(b):
                dve.wait_ge(yTh_out, b + 1)
                t = bass.ts(b, LQ)
                v.scalar_tensor_tensor(out=xTl[:, t], in0=MI[:, 0:LQ], scalar=cols[:, NW:NW + 1],
                                       in1=xTh[:, t].bitcast(F32), op0=ALU.mult, op1=ALU.subtract).then_inc(yT_out, 1)

            def router(b):
                dve.wait_ge(lgT_full, b + 1)
                v.tensor_copy(lgT[:, bass.ts(b, LQ)], MI[0:E, 0:LQ]).then_inc(lgT_out, 1)

            dve.wait_ge(x_in1, 16)
            queries(0, 0)
            row_max(0, 0, 0)

            def batch(b, k, last=False):
                later = not (isinstance(b, int) and b == 0)
                ahead = not last and not (isinstance(b, int) and b == B - 2)
                if later:
                    wait(dve, ln2, b - 1)
                row_max(2 * b + 1, k, 1)
                if later:
                    stats(b - 1, 1)
                prob_groups(2 * b)
                x1(2 * b, b, 0)
                if later:
                    moments(mv2, 1, stats2)
                if not last:
                    queries(b + 1, 1 - k)
                    row_max(2 * b + 2, 1 - k, 0)
                if ahead:
                    stats(b + 2, 0)
                prob_groups(2 * b + 1)
                x1(2 * b + 1, b, 1)
                if ahead:
                    moments(mv1[k], 0, stats1)
                if later:
                    normedT(b - 1)
                    router(b - 1)

            batch(0, 0)
            batch(1, 1)
            with dve.Fori(1, PAIRS - 1) as i:
                ch.enter(i, 2 * (4 + 4))
                batch(2 * i, 0)
                batch(2 * i + 1, 1)
            ch.leave(PAIRS - 2)
            batch(B - 2, 0)
            batch(B - 1, 1, last=True)
            dve.wait_ge(x1_out, 2 * B)
            dve.wait_ge(ln2, B - 1)
            ch.step(stats(B - 1, 1))
            moments(mv2, 1, stats2)
            normedT(B - 1)
            router(B - 1)

            dve.wait_ge(nexp, 1)
            ch.step(v.tensor_scalar(pr[:], pr[:], 1.0, None, ALU.add))
            ch.step(v.reciprocal(pr[:], pr[:]))
            mine = pr[:].unsqueeze(3).broadcast_to([P, NT, E, E])
            other = pr[:].unsqueeze(2).broadcast_to([P, NT, E, E])
            ch.step(v.tensor_tensor(rk[0][:], other, mine, ALU.is_equal))
            dve.wait_ge(low_done, 1)
            ch.step(v.tensor_tensor(rk[0][:], rk[0][:], lowi[:].unsqueeze(1).broadcast_to([P, NT, E, E]), ALU.mult))
            ch.step(v.tensor_tensor(rk[1][:], other, mine, ALU.is_gt))
            ch.step(v.tensor_tensor(rk[1][:], rk[1][:], rk[0][:], ALU.add))
            ch.step(v.tensor_reduce(rank[:], rk[1][:], AX, ALU.add))
            ch.step(v.scalar_tensor_tensor(out=comb[:], in0=rank[:], scalar=1.5, in1=pr[:], op0=ALU.is_lt, op1=ALU.mult))
            ch.step(v.tensor_reduce(den[:], comb[:], AX, ALU.add))
            ch.step(v.tensor_scalar(den[:], den[:], 1e-6, None, ALU.add))
            ch.step(v.reciprocal(den[:], den[:]))
            v.tensor_tensor(comb[:], comb[:], den[:].unsqueeze(2).broadcast_to([P, NT, E]), ALU.mult).then_inc(comb_done, 1)

            def split(c, m):
                j = m % HB
                dve.wait_ge(relu_out, BLK * c + m + 1)
                wait(dve, down_done, BLK * c + m - 3)
                v.tensor_copy(hh[j][:], rl[m % 2][:]).then_inc(hh_out, 1)
                dve.wait_ge(hh_out, BLK * c + m + 1)
                v.tensor_tensor(hl[j][:], rl[m % 2][:], hh[j][:].bitcast(F32), ALU.subtract).then_inc(split_out, 1)

            def weigh(c, e):
                dve.wait_ge(down_done, BLK * c + HB * (e + 1))
                y, w = ps[:, 4 + e % 3, :], cb[:, e, bass.ts(c, CH)]
                if e == 0:
                    v.tensor_tensor(acc[:], y, w, ALU.mult).then_inc(acc_first, 1)
                    dve.wait_ge(acc_first, c + 1)
                else:
                    wait(dve, acc_out, (E - 1) * c + e - 2)
                    v.tensor_tensor(tmp[e % 2][:], y, w, ALU.mult).then_inc(tmp_out, 1)

            def finish(c):
                dve.wait_ge(down_done, BLK * (c + 1))
                dve.wait_ge(acc_out, (E - 1) * (c + 1))
                wait(dve, finT_full, c)
                v.scalar_tensor_tensor(out=fin[:], in0=ps[:, 4 + E % 3, :], scalar=cols[:, SB2:SB2 + 1], in1=acc[:],
                                       op0=ALU.add, op1=ALU.add).then_inc(fin_out, 1)

            def store(c):
                dve.wait_ge(finT_full, c + 1)
                wait(dve, out_st, 16 * c)
                v.tensor_tensor(outs[:], MI[:].rearrange("p (t d) -> p t d", d=D),
                                xa[:, bass.ts(c, CH // P), :], ALU.add).then_inc(outs_out, 1)

            def chunk(c):
                later = not (isinstance(c, int) and c == 0)
                for m in range(BLK):
                    split(c, m)
                    if m == 3 and later:
                        finish(c - 1)
                    if m == 9 and later:
                        store(c - 1)
                    if m % HB == 3 and m > 3:
                        weigh(c, m // HB - 1)
            dve.wait_ge(cb_in0, 16)
            chunk(0)
            dve.wait_ge(cb_in1, 16 * (NC - 1))
            with dve.Fori(1, NC) as c:
                chunk(c)
            finish(NC - 1)
            store(NC - 1)


_INS = ['x', 'ctx_512', 'L0_xattn_Wq', 'L0_xattn_bq', 'L0_xattn_Wk', 'L0_xattn_bk', 'L0_xattn_Wv', 'L0_xattn_bv',
        'L0_ffn_norm_weight', 'L0_ffn_router_w', 'L0_ffn_sw1', 'L0_ffn_sb1', 'L0_ffn_sw2', 'L0_ffn_sb2',
        'L0_ffn_ew1', 'L0_ffn_eb1', 'L0_ffn_ew2', 'L0_ffn_eb2']
_OUTS = [((8, 256, 128), 'float32')]


def kernel(**inputs):
    import numpy as _np
    import concourse.bacc as _bacc
    from concourse import mybir as _mybir
    from concourse.bass_utils import run_bass_kernel_spmd as _run

    nc = _bacc.Bacc("TRN2", target_bir_lowering=False, num_devices=1)
    arrays, args = {}, []
    for name in _INS:
        a = _np.ascontiguousarray(inputs[name])
        arrays[f"in_{name}_dram"] = a
        args.append(nc.dram_tensor(f"in_{name}_dram", a.shape, _mybir.dt.from_np(a.dtype), kind="ExternalInput").ap())
    for i, (shape, dtype) in enumerate(_OUTS):
        dt = _mybir.dt.from_np(_np.dtype(dtype))
        args.append(nc.dram_tensor(f"out_{i}_dram", shape, dt, kind="ExternalOutput").ap())
    xattn_moe_kernel(nc, *args)
    r = _run(nc, [arrays], core_ids=[0])
    got = tuple(r.results[0][f"out_{i}_dram"] for i in range(len(_OUTS)))
    return got[0]
```

```python
from contextlib import ExitStack

import concourse.bass as bass
from concourse import mybir

F32 = mybir.dt.float32
F32R = mybir.dt.float32r
ALU = mybir.AluOpType
ACT = mybir.ActivationFunctionType
AX = mybir.AxisListType.X

P = 128


def wait(eng, sem, value):
    if not (isinstance(value, int) and value <= 0):
        eng.wait_ge(sem, value)


class Chain:

    def __init__(self, eng, sem):
        self.eng, self.sem, self.base, self.n = eng, sem, 0, 0

    def step(self, ins):
        ins.then_inc(self.sem, 1)
        self.n += 1
        self.eng.wait_ge(self.sem, self.base + self.n)

    def enter(self, i, per_round):
        self.first, self.per_round = self.n, per_round
        self.base = (i - 1) * per_round

    def leave(self, rounds):
        assert self.n == self.first + self.per_round, (self.n - self.first, self.per_round)
        self.base, self.n = 0, self.first + rounds * self.per_round


def xattn_moe_kernel(nc, x, ctx, Wq, bq, Wk, bk, Wv, bv, nw, router_w, sw1, sb1, sw2, sb2,
                     ew1, eb1, ew2, eb2, out):
    B, LQ, D = x.shape
    NK, KD = ctx.shape[1:]
    E, _, H = ew1.shape
    T = B * LQ
    NT = T // P
    HB = H // P
    KT = NK // P
    TAIL = NK - KT * P
    TAILE = TAIL + TAIL % 2
    NKT = KT + 1
    NE = E + 1
    CH = 512
    NC = T // CH
    BLK = NE * HB
    SH = NC * HB
    RB = E * HB
    NCOL = BLK + 4 + E
    PAIRS = B // 2
    assert D == P and LQ == 2 * P and 2 * KD == P and T % CH == 0 and B % 2 == 0

    GROUPS = [(a, min(a + 4, NKT)) for a in range(0, NKT, 4)]
    NG = len(GROUPS)

    def tile_rows(j):
        return P if j < KT else TAIL

    xt = x.rearrange("b (s p) d -> p (b s) d", p=P)
    ot = out.rearrange("b (s p) d -> p (b s) d", p=P)
    comb_d = nc.dram_tensor("comb_scratch", (E, T), F32, kind="Internal").ap()

    with ExitStack() as st:
        def sb(name, shape, dt=F32, ctx_=None):
            return (ctx_ or st).enter_context(nc.sbuf_tensor(name, shape, dt))

        def sem(name):
            return st.enter_context(nc.semaphore(name))

        xa = sb("xa", [P, NT, D])
        xTh = sb("xTh", [P, T], F32R)
        xTl = sb("xTl", [P, T], F32R)
        Wh = sb("Wh", [P, NE, 2 * H], F32R)
        Wl = sb("Wl", [P, NE, 2 * H], F32R)
        ident = sb("ident", [P, P])
        cols = sb("cols", [P, NCOL])
        B1, BQ, BK, NW, SB2, EB2 = 0, BLK, BLK + 1, BLK + 2, BLK + 3, BLK + 4
        sharedT = sb("sharedT", [P, T])
        rwTh = sb("rwTh", [P, E], F32R)
        rwTl = sb("rwTl", [P, E], F32R)

        ph1 = ExitStack()
        craw = [sb(f"craw{u}", [P, NKT, KD], F32, ph1) for u in range(2)]
        cnat = sb("cnat", [P, NKT, 2 * KD], F32R, ph1)
        cT = [sb(f"cT{u}", [P, KT * P + TAILE], F32R, ph1) for u in range(2)]
        probs = [sb(f"probs{s}", [P, NK + NK % 2], F32, ph1) for s in range(2)]
        cpv = [sb(f"cpv{u}", [P, NKT, KD], F32, ph1) for u in range(2)]
        pT = [sb(f"pT{u}", [P, NKT, LQ], F32, ph1) for u in range(2)]
        wraw = [sb(f"wraw{u}", [P, 2 * H], F32, ph1) for u in range(2)]
        xn = sb("xn", [P, 2, D], F32, ph1)
        yn = sb("yn", [P, 2, D], F32, ph1)
        xnT = sb("xnT", [P, LQ], F32, ph1)
        qh = [sb(f"qh{u}", [P, LQ], F32R, ph1) for u in range(2)]
        ql = [sb(f"ql{u}", [P, LQ], F32R, ph1) for u in range(2)]
        oT = sb("oT", [KD, LQ], F32, ph1)
        st6 = sb("st6", [P, NT, 6], F32, ph1)
        st6b = sb("st6b", [P, 2, 6], F32, ph1)
        mv1 = sb("mv1", [P, NT, 2], F32, ph1)
        rstd1 = sb("rstd1", [P, 2, NT], F32, ph1)
        mv2 = sb("mv2", [P, 2, 2], F32, ph1)
        lnt = sb("lnt", [P, 8, 2], F32, ph1)
        mhalf = sb("mhalf", [P, NT], F32, ph1)
        eps1 = sb("eps1", [P, NT], F32, ph1)
        eps2 = sb("eps2", [P, 2], F32, ph1)
        mx = sb("mx", [P, 4], F32, ph1)
        nbias = [sb(f"nbias{s}", [P, 1], F32, ph1) for s in range(2)]
        rsum = [sb(f"rsum{u}", [P, 2, 2], F32, ph1) for u in range(2)]
        rinv = sb("rinv", [P, 2, 2], F32, ph1)
        cq = [sb(f"cq{u}", [P, 2], F32, ph1) for u in range(2)]
        rows = sb("rows", [NCOL, P], F32, ph1)
        wq_s = sb("wq_s", [P, D], F32, ph1)
        wk_s = sb("wk_s", [KD, D], F32, ph1)
        wv_s = sb("wv_s", [KD, D], F32, ph1)
        rw_s = sb("rw_s", [E, D], F32, ph1)
        bvB = sb("bvB", [P, D], F32, ph1)
        wqT = sb("wqT", [P, D], F32, ph1)
        wk2T = sb("wk2T", [P, 2 * KD + 1], F32, ph1)
        wqk = sb("wqk", [P, 2 * KD + 1], F32, ph1)
        rwT = sb("rwT", [P, E], F32, ph1)
        bqk = sb("bqk", [P, 2], F32, ph1)
        bqrep = sb("bqrep", [P, P], F32, ph1)
        ph1.close()
        comb = sb("comb", [P, NT, E])
        pr = sb("pr", [P, NT, E])
        rank = sb("rank", [P, NT, E])
        den = sb("den", [P, NT])
        lowi = sb("lowi", [P, E, E])
        rl = [sb(f"rl{i}", [P, CH]) for i in range(2)]
        hh = [sb(f"hh{j}", [P, CH], F32R) for j in range(HB)]
        hl = [sb(f"hl{j}", [P, CH], F32R) for j in range(HB)]
        ph2 = ExitStack()
        rk = [sb(f"rk{i}", [P, NT, E, E], F32, ph2) for i in range(2)]
        ph2.close()
        ph3 = ExitStack()
        combT = sb("combT", [E, T], F32, ph3)
        ph3.close()
        tmp = [sb(f"tmp{i}", [P, CH]) for i in range(2)]
        fin = sb("fin", [P, CH])
        outs = sb("outs", [P, CH // P, D])
        acc = sb("acc", [P, CH])
        cb = sb("cb", [P, E, T])

        ps = st.enter_context(nc.psum_tensor("ps", [P, 8, 512], F32))
        S = ps[:, 0:4, :].rearrange("p a b -> p (a b)")
        PT = [ps[:, 4, :], ps[:, 5, :]]
        PV = ps[0:KD, 6, 0:LQ]
        MI = ps[:, 7, :]

        x_in0, x_in1, setup_in = sem("x_in0"), sem("x_in1"), sem("setup_in")
        ctx_in = [sem("ctx_in0"), sem("ctx_in1")]
        cpv_in = [sem("cpv_in0"), sem("cpv_in1")]
        w_in = [sem("w_in0"), sem("w_in1")]
        consts = sem("consts")
        setT, setT_out = sem("setT"), sem("setT_out")
        setM, setM_out = sem("setM"), sem("setM_out")
        c_hi, w_hi = sem("c_hi"), sem("w_hi")
        c_split = sem("c_split")
        w_split = sem("w_split")
        pool_chain, dve_chain = sem("pool_chain"), sem("dve_chain")
        stats1, stats2_out = sem("stats1"), sem("stats2_out")
        ln1, ln2 = sem("ln1"), sem("ln2")
        cT_full, cT_out = sem("cT_full"), sem("cT_out")
        xnT_full, xnT_out = sem("xnT_full"), sem("xnT_out")
        q_full, qh_out, q_out = sem("q_full"), sem("qh_out"), sem("q_out")
        s_done = sem("s_done")
        bias_done = sem("bias_done")
        exp_done = sem("exp_done")
        pt_full = sem("pt_full")
        pt0_out, pt1_out = sem("pt0_out"), sem("pt1_out")
        pv_done, oT_out = sem("pv_done"), sem("oT_out")
        o_done, x1_out = sem("o_done"), sem("x1_out")
        yT_full, yTh_out, yT_out = sem("yT_full"), sem("yTh_out"), sem("yT_out")
        lg_full = sem("lg_full")
        xb_out, bqk_out, rinv_out = sem("xb_out"), sem("bqk_out"), sem("rinv_out")
        nexp, comb_done, combT_full, combT_out = sem("nexp"), sem("comb_done"), sem("combT_full"), sem("combT_out")
        comb_st, cb_in0, cb_in1 = sem("comb_st"), sem("cb_in0"), sem("cb_in1")
        equal_out, ties_out = sem("equal_out"), sem("ties_out")
        up_done, relu_out, hh_out, split_out = sem("up_done"), sem("relu_out"), sem("hh_out"), sem("split_out")
        down_done = sem("down_done")
        shared_out, tmp_out, acc_out = sem("shared_out"), sem("tmp_out"), sem("acc_out")
        finT_full, outs_out, out_st = sem("finT_full"), sem("outs_out"), sem("out_st")

        PROJECT_AT, YT_AT, LOGITS_AT, TIES_AT, COMB_AT = 1, 7, 8, 12, (4, 6, 8, 10)

        block = st.enter_context(nc.Block())

        @block.sync
        def _(sp):
            def load_keys(dst, b, done):
                nc.sync.dma_start(dst[:, 0:KT, :], ctx[b, 0:KT * P, :].rearrange("(p j) d -> p j d", j=KT)).then_inc(done, 16)
                nc.sync.dma_start(dst[0:TAIL, KT, :], ctx[b, KT * P:NK, :]).then_inc(done, 16)

            def load_weights(w1, w2, u):
                nc.sync.dma_start(wraw[u][:, 0:H], w1).then_inc(w_in[u], 16)
                nc.sync.dma_start(wraw[u][:, H:2 * H].rearrange("p (j o) -> p j o", j=HB),
                                  w2.rearrange("(j p) o -> p j o", p=P)).then_inc(w_in[u], 16)

            nc.sync.dma_start(xa[:, 0:4, :], xt[:, 0:4, :]).then_inc(x_in0, 16)
            nc.sync.dma_start(wq_s[:], Wq).then_inc(setup_in, 16)
            nc.sync.dma_start(wk_s[:], Wk).then_inc(setup_in, 16)
            nc.sync.dma_start(rows[0:E * HB, :], eb1.rearrange("e (j p) -> (e j) p", p=P)).then_inc(setup_in, 16)
            nc.sync.dma_start(rows[E * HB:BLK, :], sb1.rearrange("(j p) -> j p", p=P)).then_inc(setup_in, 16)
            for r, v in ((BQ, bq), (BK, bk), (NW, nw), (SB2, sb2)):
                nc.sync.dma_start(rows[r:r + 1, :], v.rearrange("(a p) -> a p", a=1)).then_inc(setup_in, 16)
            nc.sync.dma_start(rw_s[:], router_w).then_inc(setup_in, 16)
            nc.sync.dma_start(wv_s[:], Wv).then_inc(setup_in, 16)
            nc.sync.dma_start(bvB[:], bv.partition_broadcast(P)).then_inc(setup_in, 16)
            nc.sync.dma_start(rows[EB2:NCOL, :], eb2).then_inc(setup_in, 16)
            sp.wait_ge(consts, 1)
            load_keys(craw[0], 0, ctx_in[0])
            load_keys(craw[1], 1, ctx_in[1])
            nc.sync.dma_start(xa[:, 4:NT, :], xt[:, 4:NT, :]).then_inc(x_in1, 16)
            load_weights(sw1, sw2, 0)
            load_weights(ew1[0], ew2[0], 1)
            load_keys(cpv[0], 0, cpv_in[0])
            load_keys(cpv[1], 1, cpv_in[1])

            def batch(b, u, last):
                if not last:
                    wait(sp, c_split, b + 1)
                    load_keys(craw[u], b + 2, ctx_in[u])
                if not (last and u == 1):
                    wait(sp, w_split, b + 1)
                    load_weights(ew1[b + 1], ew2[b + 1], u)
                if not (isinstance(b, int) and (b == 0 or b == B - 1)):
                    wait(sp, pv_done, b)
                    load_keys(cpv[1 - u], b + 1, cpv_in[1 - u])

            batch(0, 0, False)
            batch(1, 1, False)
            with sp.Fori(1, PAIRS - 1) as i:
                batch(2 * i, 0, False)
                batch(2 * i + 1, 1, False)
            batch(B - 2, 0, True)
            batch(B - 1, 1, True)

            sp.wait_ge(w_split, NE)
            for c in range(NC):
                sp.wait_ge(combT_out, c + 1)
                t = slice(c * CH, (c + 1) * CH)
                nc.sync.dma_start(comb_d[:, t], combT[:, t]).then_inc(comb_st, 16)
                sp.wait_ge(comb_st, 16 * (c + 1))
                nc.sync.dma_start(cb[:, :, t], comb_d[:, t].partition_broadcast(P)).then_inc(
                    cb_in0 if c == 0 else cb_in1, 16)
            with sp.Fori(0, NC) as c:
                sp.wait_ge(outs_out, c + 1)
                nc.sync.dma_start(ot[:, bass.ts(c, CH // P), :], outs[:]).then_inc(out_st, 16)
            sp.wait_ge(out_st, 16 * NC)

        @block.gpsimd
        def _(pool):
            ch = Chain(pool, pool_chain)
            gp = nc.gpsimd

            gp.memset(craw[0][:, KT, :], 0.0)
            gp.memset(craw[1][:, KT, :], 0.0).then_inc(consts, 1)
            ch.step(gp.memset(ident[:], 0.0))
            gp.affine_select(out=ident[:], in_=ident[:], compare_op=ALU.not_equal, fill=1.0, base=0,
                             pattern=[[-1, P]], channel_multiplier=1).then_inc(consts, 1)
            gp.memset(eps1[:], 1e-5)
            gp.memset(eps2[:], 1e-8)
            ch.step(gp.memset(mhalf[:], -0.5))

            def split_ctx(b, k):
                pool.wait_ge(c_hi, b + 1)
                gp.tensor_tensor(cnat[:, :, KD:2 * KD], craw[k][:], cnat[:, :, 0:KD].bitcast(F32),
                                 ALU.subtract).then_inc(c_split, 1)

            def split_weights(n, e, u):
                pool.wait_ge(w_hi, n + 1)
                gp.tensor_tensor(Wl[:, e, :], wraw[u][:], Wh[:, e, :].bitcast(F32), ALU.subtract).then_inc(w_split, 1)

            def norm1(b):
                wait(pool, xnT_full, b)
                t = bass.ts(b, 2)
                ch.step(gp.tensor_tensor(xn[:], xa[:, t, :], mv1[:, t, 0:1].broadcast_to([P, 2, D]), ALU.subtract))
                gp.tensor_tensor(xn[:], xn[:], rstd1[:, 1, t].unsqueeze(2).broadcast_to([P, 2, D]),
                                 ALU.mult).then_inc(ln1, 1)
                gp.tensor_tensor(xa[:, t, :], xa[:, t, :],
                                 bvB[:].unsqueeze(1).broadcast_to([P, 2, D]), ALU.add).then_inc(xb_out, 1)

            def norm2(b):
                pool.wait_ge(stats2_out, b + 1)
                wait(pool, yT_full, b)
                gp.tensor_tensor(lnt[:, 2, :], mv2[:, :, 1], eps1[:, 0:2], ALU.add)
                ch.step(gp.tensor_tensor(yn[:], xa[:, bass.ts(b, 2), :],
                                         mv2[:, :, 0].unsqueeze(2).broadcast_to([P, 2, D]), ALU.subtract))
                ch.step(gp.tensor_tensor(lnt[:, 3, :], lnt[:, 2, :], mhalf[:, 0:2], ALU.pow))
                ch.step(gp.tensor_tensor(lnt[:, 4, :], mv2[:, :, 1], lnt[:, 3, :], ALU.mult))
                ch.step(gp.tensor_tensor(lnt[:, 5, :], lnt[:, 4, :], lnt[:, 3, :], ALU.mult))
                ch.step(gp.tensor_tensor(lnt[:, 6, :], lnt[:, 5, :], eps2[:], ALU.add))
                ch.step(gp.tensor_tensor(lnt[:, 7, :], lnt[:, 6, :], mhalf[:, 0:2], ALU.pow))
                ch.step(gp.tensor_tensor(lnt[:, 0, :], lnt[:, 7, :], lnt[:, 3, :], ALU.mult))
                gp.tensor_tensor(yn[:], yn[:], lnt[:, 0, :].unsqueeze(2).broadcast_to([P, 2, D]),
                                 ALU.mult).then_inc(ln2, 1)

            split_ctx(0, 0)
            pool.wait_ge(stats1, 1)
            ch.step(gp.tensor_tensor(rstd1[:, 0, :], mv1[:, :, 1], eps1[:], ALU.add))
            ch.step(gp.tensor_tensor(rstd1[:, 1, :], rstd1[:, 0, :], mhalf[:], ALU.pow))
            pool.wait_ge(setup_in, 16 * 12)
            norm1(0)
            split_ctx(1, 1)
            norm1(1)

            def cycle(b, k):
                if not (isinstance(b, int) and b >= B - 2):
                    norm1(b + 2)
                if not (isinstance(b, int) and b < 2):
                    norm2(b - 2)
                split_weights(b, E if isinstance(b, int) and b == 0 else b - 1, k)
                if not (isinstance(b, int) and b >= B - 2):
                    split_ctx(b + 2, k)

            cycle(0, 0)
            cycle(1, 1)
            with pool.Fori(1, PAIRS - 1) as i:
                ch.enter(i, 2 * (1 + 7))
                cycle(2 * i, 0)
                cycle(2 * i + 1, 1)
            ch.leave(PAIRS - 2)
            cycle(B - 2, 0)
            cycle(B - 1, 1)
            split_weights(B, B - 1, 0)
            norm2(B - 2)
            norm2(B - 1)
            pool.wait_ge(yT_full, B)
            ch.step(gp.memset(lowi[:], 1.0))
            ch.step(gp.affine_select(out=lowi[:], in_=lowi[:], compare_op=ALU.is_gt, fill=0.0, base=0,
                                     pattern=[[1, E], [-1, E]], channel_multiplier=0))
            pool.wait_ge(equal_out, 1)
            gp.tensor_tensor(rk[0][:], rk[0][:], lowi[:].unsqueeze(1).broadcast_to([P, NT, E, E]),
                             ALU.mult).then_inc(ties_out, 1)

            def sums(c):
                for e in range(E):
                    pool.wait_ge(tmp_out, E * c + e + 1)
                    if e == E - 1:
                        wait(pool, finT_full, c)
                    src = sharedT[:, bass.ts(c, CH)] if e == 0 else acc[:]
                    dst = fin[:] if e == E - 1 else acc[:]
                    gp.tensor_tensor(dst, src, tmp[e % 2][:], ALU.add).then_inc(acc_out, 1)
                    pool.wait_ge(acc_out, E * c + e + 1)
            pool.wait_ge(shared_out, NC)
            sums(0)
            with pool.Fori(1, NC) as c:
                sums(c)

        @block.scalar
        def _(act):
            a = nc.scalar

            act.wait_ge(setT, 4)
            a.copy(wqT[:], ps[:, 0, 0:D]).then_inc(setT_out, 1)
            a.copy(cols[:], ps[:, 2, 0:NCOL]).then_inc(setT_out, 1)
            a.copy(rwT[:], ps[:, 3, 0:E]).then_inc(setT_out, 1)
            act.wait_ge(setM, 3)
            a.copy(wqk[:], ps[:, 0, 0:2 * KD + 1]).then_inc(setM_out, 1)

            def ctx_groups(b, k, gs):
                for g in gs:
                    j0, j1 = GROUPS[g]
                    act.wait_ge(cT_full, NG * b + g + 1)
                    w = (j1 - j0) * P if j1 <= KT else TAILE
                    a.copy(cT[k][:, j0 * P:j0 * P + w], PT[g % 2][:, 0:w]).then_inc(cT_out, 1)

            def queriesT(b):
                act.wait_ge(xnT_full, b + 1)
                a.copy(xnT[:], MI[:, 0:LQ]).then_inc(xnT_out, 1)

            def queries(b, k):
                act.wait_ge(q_full, b + 1)
                a.activation(qh[k][:], MI[:, 0:LQ], ACT.Identity, bias=bqk[:, 0:1]).then_inc(qh_out, 1)

            def ctx_hi(b, k):
                wait(act, ctx_in[k], (b + (2 - k)) * 16)
                wait(act, cT_full, NG * b)
                a.copy(cnat[:, :, 0:KD], craw[k][:]).then_inc(c_hi, 1)

            def weights_hi(n, e, u):
                wait(act, w_in[u], (n + (2 - u)) * 16)
                a.copy(Wh[:, e, :], wraw[u][:]).then_inc(w_hi, 1)

            def exps(g, k, s):
                act.wait_ge(bias_done, g + 1)
                a.activation(probs[s][:, 0:1024], S[:, 0:1024], ACT.Exp, bias=nbias[s][:],
                             accum_out=rsum[k][:, s, 0:1]).then_inc(exp_done, 1)
                a.activation(probs[s][:, 1024:NK], S[:, 1024:NK], ACT.Exp, bias=nbias[s][:],
                             accum_out=rsum[k][:, s, 1:2]).then_inc(exp_done, 1)

            def prob_groups(b, k, ns):
                for n in ns:
                    j0, j1 = GROUPS[n]
                    act.wait_ge(pt_full, NG * (2 * b + 1) + n + 1)
                    r = tile_rows(j1 - 1)
                    a.copy(pT[k][0:r, j0:j1, P:2 * P],
                           PT[n % 2][0:r, 0:(j1 - j0) * P].rearrange("p (a b) -> p a b", b=P)).then_inc(pt1_out, 1)

            def attn_out(b):
                act.wait_ge(pv_done, b + 1)
                a.copy(oT[:], PV).then_inc(oT_out, 1)

            def normedT(b):
                act.wait_ge(yT_full, b + 1)
                a.activation(xTh[:, bass.ts(b, LQ)], MI[:, 0:LQ], ACT.Copy, scale=cols[:, NW:NW + 1]).then_inc(yTh_out, 1)

            ctx_hi(0, 0)
            ctx_groups(0, 0, range(NG))
            ctx_hi(1, 1)
            act.wait_ge(bqk_out, 1)
            queriesT(0)
            queries(0, 0)
            queriesT(1)
            queries(1, 1)
            exps(0, 0, 0)

            def cycle(b, k):
                first = isinstance(b, int) and b == 0
                last = isinstance(b, int) and b == B - 1
                more = not (isinstance(b, int) and b >= B - 2)
                if not last:
                    ctx_groups(b + 1, 1 - k, (0, 1))
                exps(2 * b + 1, k, 1)
                if more:
                    queriesT(b + 2)
                if not last:
                    ctx_groups(b + 1, 1 - k, (2, 3))
                weights_hi(b, E if first else b - 1, k)
                if more:
                    queries(b + 2, k)
                prob_groups(b, k, (0, 1))
                if not last:
                    exps(2 * b + 2, 1 - k, 0)
                if more:
                    ctx_hi(b + 2, k)
                prob_groups(b, k, (2, 3))
                if not first:
                    attn_out(b - 1)
                if not (isinstance(b, int) and b < 2):
                    normedT(b - 2)

            cycle(0, 0)
            cycle(1, 1)
            with act.Fori(1, PAIRS - 1) as i:
                cycle(2 * i, 0)
                cycle(2 * i + 1, 1)
            cycle(B - 2, 0)
            cycle(B - 1, 1)
            weights_hi(B, B - 1, 0)
            attn_out(B - 1)
            normedT(B - 2)

            def relu_shared(n):
                j, bias = n % HB, cols[:, B1 + RB + n % HB:B1 + RB + n % HB + 1]
                act.wait_ge(up_done, n + 1)
                wait(act, down_done, n - 3)
                a.activation(hh[j][:], ps[:, j, :], ACT.Relu, bias=bias)
                wait(act, split_out, n - 1)
                a.activation(rl[n % 2][:], ps[:, j, :], ACT.Relu, bias=bias).then_inc(relu_out, 1)

            def shared(c):
                act.wait_ge(down_done, HB * (c + 1))
                a.activation(sharedT[:, c * CH:(c + 1) * CH], ps[:, 4 + c % 2, :], ACT.Identity,
                             bias=cols[:, SB2:SB2 + 1]).then_inc(shared_out, 1)

            def relu(c, m):
                act.wait_ge(up_done, SH + RB * c + m + 1)
                act.wait_ge(split_out, SH + RB * c + m - 1)
                a.activation(rl[m % 2][:], ps[:, m % HB, :], ACT.Relu, bias=cols[:, B1 + m:B1 + m + 1]).then_inc(relu_out, 1)

            for n in range(SH):
                relu_shared(n)
                if n % HB == HB - 1 and n > HB:
                    shared(n // HB - 1)
                if n == YT_AT:
                    normedT(B - 1)
                if n == LOGITS_AT:
                    act.wait_ge(lg_full, 1)
                    a.activation(pr[:].rearrange("p t e -> p (t e)"), MI[:, LQ:LQ + NT * E], ACT.Exp,
                                 scale=-1.0).then_inc(nexp, 1)
            for m in range(RB):
                relu(0, m)
                if m == HB - 1:
                    shared(NC - 1)
                if m in COMB_AT:
                    g = COMB_AT.index(m)
                    act.wait_ge(combT_full, g + 1)
                    a.copy(combT[:, g * CH:(g + 1) * CH], MI[0:E, :]).then_inc(combT_out, 1)
            with act.Fori(1, NC) as c:
                for m in range(RB):
                    relu(c, m)

        @block.tensor
        def _(pe):
            mm, tr = nc.tensor.matmul, nc.tensor.transpose

            pe.wait_ge(consts, 2)
            pe.wait_ge(setup_in, 16 * 12)
            tr(ps[:, 0, 0:D], wq_s[:], ident[:]).then_inc(setT, 1)
            tr(ps[:, 1, 0:KD], wk_s[:], ident[0:KD, 0:KD]).then_inc(setT, 1)
            tr(ps[:, 2, 0:NCOL], rows[:], ident[0:NCOL, 0:NCOL]).then_inc(setT, 1)
            tr(ps[:, 3, 0:E], rw_s[:], ident[0:E, 0:E]).then_inc(setT, 1)
            pe.wait_ge(setT_out, 6)
            mm(ps[:, 0, 0:2 * KD + 1], wqT[:], wk2T[:], start=True, stop=True).then_inc(setM, 1)
            mm(ps[:, 1, 0:1], wk2T[:, 0:2 * KD], cols[:, BQ:BQ + 1], start=True, stop=True).then_inc(setM, 1)
            mm(ps[:, 2, 0:1], bqrep[:], cols[:, BK:BK + 1], start=True, stop=True).then_inc(setM, 1)

            def ctx_groups(b, gs):
                for g in gs:
                    j0, j1 = GROUPS[g]
                    if g == 0:
                        pe.wait_ge(c_split, b + 1)
                    if isinstance(b, int) and (b == 0 or b == 1 and g < 2):
                        wait(pe, cT_out, NG * b + g - 1)
                    elif g < 2:
                        pe.wait_ge(pt1_out, NG * (b - 1) - 1 + g)
                    else:
                        pe.wait_ge(pt0_out, NG * (b - 1) + g + 1)
                    for j in range(j0, j1):
                        r = P if j < KT else TAILE
                        last = tr(PT[g % 2][:, (j - j0) * P:(j - j0) * P + r],
                                  cnat[0:r, j, :].bitcast(F32), ident[0:r, 0:r])
                    last.then_inc(cT_full, 1)

            def queriesT(b):
                pe.wait_ge(ln1, b + 1)
                wait(pe, x1_out, b - 3)
                wait(pe, q_out, b)
                for s in range(2):
                    last = tr(MI[:, s * P:(s + 1) * P], xn[:, s, :], ident[:])
                last.then_inc(xnT_full, 1)

            def queries(b):
                pe.wait_ge(xnT_out, b + 1)
                mm(MI[:, 0:LQ], wqk[:, 0:2 * KD], xnT[:], start=True, stop=True)
                for s in range(2):
                    last = mm(MI[:, LQ + s:LQ + s + 1], xnT[:, s * P:(s + 1) * P], wqk[:, 2 * KD:2 * KD + 1],
                              start=True, stop=True)
                last.then_inc(q_full, 1)

            def scores(g, b, k, s):
                if s == 0:
                    pe.wait_ge(q_out, b + 1)
                for n, (j0, j1) in enumerate(GROUPS):
                    if n % 2 == 0:
                        wait(pe, exp_done, 2 * g - 1 + n // 2)
                    if s == 0:
                        pe.wait_ge(cT_out, NG * b + n + 1)
                    a0 = j0 * P
                    w = (j1 - j0) * P if j1 <= KT else TAILE
                    mm(S[:, a0:a0 + w], qh[k][:, s * P:(s + 1) * P], cT[k][:, a0:a0 + w], start=True, stop=False)
                    last = mm(S[:, a0:a0 + w], ql[k][:, s * P:(s + 1) * P], cT[k][:, a0:a0 + w], start=False, stop=True)
                    if n % 2 == 1:
                        last.then_inc(s_done, 1)

            def turns(b, k, s, ns):
                mine, other = (pt0_out, pt1_out) if s == 0 else (pt1_out, pt0_out)
                for n in ns:
                    j0, j1 = GROUPS[n]
                    if n % 2 == 0:
                        pe.wait_ge(exp_done, 2 * (2 * b + s) + n // 2 + 1)
                    if n >= 2:
                        pe.wait_ge(mine, NG * b + n - 1)
                    elif not (isinstance(b, int) and b == B - 1):
                        pe.wait_ge(cT_out, NG * (b + 1) + 2 * s + n + 1)
                    else:
                        pe.wait_ge(other, NG * (b + s) - 1 + n)
                    for j in range(j0, j1):
                        r = tile_rows(j)
                        last = tr(PT[n % 2][0:r, (j - j0) * P:(j - j0 + 1) * P],
                                  probs[s][:, j * P:j * P + r], ident[:])
                    last.then_inc(pt_full, 1)

            def attend(b, k, j0, j1):
                if j0 == 0:
                    pe.wait_ge(pt0_out, NG * (b + 1))
                    pe.wait_ge(pt1_out, NG * (b + 1))
                    pe.wait_ge(cpv_in[k], (b + 2 - k) * 16)
                    wait(pe, oT_out, b)
                for j in range(j0, j1):
                    r = tile_rows(j)
                    last = mm(PV, cpv[k][0:r, j, :], pT[k][0:r, j, :], start=(j == 0), stop=(j == NKT - 1))
                if j1 == NKT:
                    last.then_inc(pv_done, 1)

            def project(b):
                pe.wait_ge(oT_out, b + 1)
                wait(pe, yT_out, b)
                pe.wait_ge(q_out, min(b + 4, B) if isinstance(b, int) else b + 4)
                for s in range(2):
                    last = mm(MI[:, s * P:(s + 1) * P], oT[:, s * P:(s + 1) * P], wv_s[:], start=True, stop=True)
                last.then_inc(o_done, 1)

            def normedT(b, queries_read, projections_read):
                pe.wait_ge(ln2, b + 1)
                pe.wait_ge(q_out, queries_read)
                pe.wait_ge(x1_out, projections_read)
                wait(pe, yT_out, b)
                for s in range(2):
                    last = tr(MI[:, s * P:(s + 1) * P], yn[:, s, :], ident[:])
                last.then_inc(yT_full, 1)

            def router():
                pe.wait_ge(yT_out, B)
                for t in range(NT):
                    lg, x_t = MI[:, LQ + t * E:LQ + (t + 1) * E], slice(t * P, (t + 1) * P)
                    mm(lg, xTh[:, x_t], rwTh[:], start=True, stop=False)
                    mm(lg, xTl[:, x_t], rwTh[:], start=False, stop=False)
                    last = mm(lg, xTh[:, x_t], rwTl[:], start=False, stop=True)
                last.then_inc(lg_full, 1)

            ctx_groups(0, range(NG))
            pe.wait_ge(setM_out, 1)
            pe.wait_ge(bqk_out, 1)
            for b in range(2):
                queriesT(b)
                queries(b)
                if b == 0:
                    scores(0, 0, 0, 0)

            def cycle(b, k):
                first = isinstance(b, int) and b == 0
                last = isinstance(b, int) and b == B - 1
                more = not (isinstance(b, int) and b >= B - 2)
                later = not (isinstance(b, int) and b < 2)

                def attend_before(j0, j1):
                    if not first:
                        attend(b - 1, 1 - k, j0, j1)
                scores(2 * b + 1, b, k, 1)
                if not last:
                    ctx_groups(b + 1, (0, 1))
                attend_before(0, 2)
                if later:
                    project(b - 2)
                attend_before(2, 4)
                turns(b, k, 0, (0, 1))
                attend_before(4, 6)
                turns(b, k, 0, (2, 3))
                if more:
                    queriesT(b + 2)
                attend_before(6, 7)
                if not last:
                    ctx_groups(b + 1, (2, 3))
                    scores(2 * b + 2, b + 1, 1 - k, 0)
                if more:
                    queries(b + 2)
                turns(b, k, 1, (0, 1))
                attend_before(7, 10)
                turns(b, k, 1, (2, 3))
                attend_before(10, NKT)
                if later:
                    normedT(b - 2, b + 3 if more else B, b - 1)

            cycle(0, 0)
            cycle(1, 1)
            with pe.Fori(1, PAIRS - 1) as i:
                cycle(2 * i, 0)
                cycle(2 * i + 1, 1)
            cycle(B - 2, 0)
            cycle(B - 1, 1)
            project(B - 2)
            attend(B - 1, 1, 0, NKT)
            normedT(B - 2, B, B - 1)

            LAG = 3

            def up(n, e, j, xs):
                wait(pe, relu_out, n - 3)
                w = slice(j * P, (j + 1) * P)
                mm(ps[:, j, :], Wh[:, e, w], xTh[:, xs], start=True, stop=False)
                mm(ps[:, j, :], Wh[:, e, w], xTl[:, xs], start=False, stop=False)
                mm(ps[:, j, :], Wl[:, e, w], xTh[:, xs], start=False, stop=True).then_inc(up_done, 1)

            def down(n, e, j, y):
                pe.wait_ge(split_out, n + 1)
                w = slice(H + j * P, H + (j + 1) * P)
                mm(ps[:, y, :], Wh[:, e, w], hh[j][:], start=(j == 0), stop=False)
                mm(ps[:, y, :], Wl[:, e, w], hh[j][:], start=False, stop=False)
                last = mm(ps[:, y, :], Wh[:, e, w], hl[j][:], start=False, stop=(j == HB - 1))
                last.then_inc(down_done, 1)

            def down_shared(n):
                c = n // HB
                if n % HB == 0:
                    wait(pe, shared_out, c - 1)
                down(n, E, n % HB, 4 + c % 2)

            def down_routed(c, m):
                e, j = m // HB, m % HB
                if j == 0:
                    if e >= 3:
                        pe.wait_ge(tmp_out, E * c + e - 2)
                    elif isinstance(c, int) and c == 0:
                        pe.wait_ge(shared_out, min(3 + e, NC))
                    else:
                        pe.wait_ge(tmp_out, E * (c - 1) + LAST_IN[e] + 1)
                down(SH + RB * c + m, e, j, 4 + e % 3)

            LAST_IN = [max(f for f in range(E) if f % 3 == e) for e in range(3)]

            def out_transposes(c):
                pe.wait_ge(acc_out, E * (c + 1))
                wait(pe, outs_out, c)
                for t in range(CH // P):
                    last = tr(MI[:, t * P:(t + 1) * P], fin[:, t * P:(t + 1) * P], ident[:])
                last.then_inc(finT_full, 1)

            def comb_rows(g):
                pe.wait_ge(comb_done, 1)
                wait(pe, combT_out, g)
                for t in range(CH // P):
                    last = tr(MI[0:E, t * P:(t + 1) * P], comb[:, g * (CH // P) + t, :], ident[:])
                last.then_inc(combT_full, 1)

            pe.wait_ge(w_split, NE)
            for n in range(SH):
                up(n, E, n % HB, slice(n // HB * CH, (n // HB + 1) * CH))
                if n >= LAG:
                    down_shared(n - LAG)
                if n == PROJECT_AT:
                    project(B - 1)
                if n == YT_AT:
                    normedT(B - 1, B, B)
                if n == LOGITS_AT:
                    router()

            def chunk(c):
                for m in range(RB):
                    up(SH + RB * c + m, m // HB, m % HB, bass.ts(c, CH))
                    if m >= LAG:
                        down_routed(c, m - LAG)
                    elif isinstance(c, int) and c == 0:
                        down_shared(SH + m - LAG)
                    else:
                        down_routed(c - 1, RB + m - LAG)
                    if isinstance(c, int) and c == 0:
                        if m in COMB_AT:
                            comb_rows(COMB_AT.index(m))
                    elif m == 8:
                        out_transposes(c - 1)
            chunk(0)
            pe.wait_ge(combT_out, NC)
            with pe.Fori(1, NC) as c:
                chunk(c)
            for m in range(RB - LAG, RB):
                down_routed(NC - 1, m)
            out_transposes(NC - 1)

        @block.vector
        def _(dve):
            v = nc.vector
            ch = Chain(dve, dve_chain)

            def stats2(b):
                for s in range(2):
                    last = v.bn_stats(st6b[:, s, :], xa[:, 2 * b + s, :])
                return last

            def moments2():
                for s in range(2):
                    last = v.bn_aggr(mv2[:, s, :], st6b[:, s, :])
                last.then_inc(stats2_out, 1)

            dve.wait_ge(x_in0, 16)
            dve.wait_ge(x_in1, 16)
            for t in range(NT):
                last = v.bn_stats(st6[:, t, :], xa[:, t, :])
            ch.step(last)
            for t in range(NT):
                last = v.bn_aggr(mv1[:, t, :], st6[:, t, :])
            last.then_inc(stats1, 1)

            dve.wait_ge(setT, 4)
            v.tensor_copy(wk2T[:, 0:KD], ps[:, 1, 0:KD])
            v.tensor_copy(wk2T[:, KD:2 * KD], ps[:, 1, 0:KD]).then_inc(setT_out, 1)
            dve.wait_ge(setT_out, 4)
            v.tensor_copy(wk2T[:, 2 * KD:2 * KD + 1], cols[:, BK:BK + 1]).then_inc(setT_out, 1)
            v.tensor_copy(bqrep[:], cols[:, BQ:BQ + 1].broadcast_to([P, P])).then_inc(setT_out, 1)
            ch.step(v.tensor_copy(rwTh[:], rwT[:]))
            ch.step(v.tensor_tensor(rwTl[:], rwT[:], rwTh[:].bitcast(F32), ALU.subtract))
            dve.wait_ge(setM, 3)
            v.tensor_copy(bqk[:, 0:1], ps[:, 1, 0:1])
            v.tensor_copy(bqk[:, 1:2], ps[:, 2, 0:1]).then_inc(bqk_out, 1)
            dve.wait_ge(bqk_out, 1)

            def queries(b, k):
                dve.wait_ge(qh_out, b + 1)
                v.scalar_tensor_tensor(out=ql[k][:], in0=MI[:, 0:LQ], scalar=bqk[:, 0:1], in1=qh[k][:].bitcast(F32),
                                       op0=ALU.add, op1=ALU.subtract)
                v.tensor_scalar(cq[k][:], MI[:, LQ:LQ + 2], bqk[:, 1:2], None, ALU.add).then_inc(q_out, 1)

            def row_max(g, k, s):
                dve.wait_ge(s_done, 2 * g + 1)
                v.tensor_reduce(mx[:, 0:1], S[:, 0:1024], AX, ALU.max)
                dve.wait_ge(s_done, 2 * g + 2)
                ch.step(v.tensor_reduce(mx[:, 1:2], S[:, 1024:NK], AX, ALU.max))
                ch.step(v.scalar_tensor_tensor(out=mx[:, 2:3], in0=mx[:, 0:1], scalar=mx[:, 1:2],
                                               in1=cq[k][:, s:s + 1], op0=ALU.max, op1=ALU.add))
                v.scalar_tensor_tensor(out=nbias[s][:], in0=mx[:, 2:3], scalar=-1.0, in1=cq[k][:, s:s + 1],
                                       op0=ALU.mult, op1=ALU.add).then_inc(bias_done, 1)

            def prob_groups(b, k, ns):
                for n in ns:
                    j0, j1 = GROUPS[n]
                    dve.wait_ge(pt_full, NG * 2 * b + n + 1)
                    r = tile_rows(j1 - 1)
                    v.tensor_copy(pT[k][0:r, j0:j1, 0:P],
                                  PT[n % 2][0:r, 0:(j1 - j0) * P].rearrange("p (a b) -> p a b", b=P)).then_inc(pt0_out, 1)

            def row_sums(b, k):
                dve.wait_ge(exp_done, 4 * b + 4)
                ch.step(v.tensor_tensor(rinv[:, 0, :], rsum[k][:, :, 0], rsum[k][:, :, 1], ALU.add))
                v.reciprocal(rinv[:, 1, :], rinv[:, 0, :]).then_inc(rinv_out, 1)

            def x1(b):
                dve.wait_ge(rinv_out, b + 1)
                dve.wait_ge(xb_out, b + 1)
                dve.wait_ge(o_done, b + 1)
                for s in range(2):
                    last = v.scalar_tensor_tensor(out=xa[:, 2 * b + s, :], in0=MI[:, s * P:(s + 1) * P],
                                                  scalar=rinv[:, 1, s:s + 1], in1=xa[:, 2 * b + s, :],
                                                  op0=ALU.mult, op1=ALU.add)
                last.then_inc(x1_out, 1)
                dve.wait_ge(x1_out, b + 1)

            def normedT(b):
                dve.wait_ge(yTh_out, b + 1)
                t = bass.ts(b, LQ)
                v.scalar_tensor_tensor(out=xTl[:, t], in0=MI[:, 0:LQ], scalar=cols[:, NW:NW + 1],
                                       in1=xTh[:, t].bitcast(F32), op0=ALU.mult, op1=ALU.subtract).then_inc(yT_out, 1)

            queries(0, 0)
            row_max(0, 0, 0)
            queries(1, 1)

            def cycle(b, k):
                later = not (isinstance(b, int) and b < 2)
                if later:
                    x1(b - 2)
                if not (isinstance(b, int) and b == 0):
                    row_sums(b - 1, 1 - k)
                if later:
                    ch.step(stats2(b - 2))
                    wait(dve, ln2, b - 2)
                prob_groups(b, k, (0,))
                if later:
                    moments2()
                prob_groups(b, k, (1, 2, 3))
                if not (isinstance(b, int) and b == B - 1):
                    row_max(2 * b + 2, 1 - k, 0)
                if not (isinstance(b, int) and b >= B - 2):
                    queries(b + 2, k)
                if not (isinstance(b, int) and b == B - 1):
                    row_max(2 * b + 3, 1 - k, 1)
                if later:
                    normedT(b - 2)

            row_max(1, 0, 1)
            cycle(0, 0)
            cycle(1, 1)
            with dve.Fori(1, PAIRS - 1) as i:
                ch.enter(i, 2 * (4 + 2))
                cycle(2 * i, 0)
                cycle(2 * i + 1, 1)
            ch.leave(PAIRS - 2)
            cycle(B - 2, 0)
            cycle(B - 1, 1)

            def last_x1(b):
                x1(b)
                if b == B - 2:
                    row_sums(B - 1, 1)
                ch.step(stats2(b))
                dve.wait_ge(ln2, b)
                moments2()

            def split_shared(n):
                dve.wait_ge(relu_out, n + 1)
                v.tensor_tensor(hl[n % HB][:], rl[n % 2][:], hh[n % HB][:].bitcast(F32),
                                ALU.subtract).then_inc(split_out, 1)

            def split(c, m):
                j = m % HB
                dve.wait_ge(relu_out, SH + RB * c + m + 1)
                dve.wait_ge(down_done, SH + RB * c + m - 3)
                v.tensor_copy(hh[j][:], rl[m % 2][:]).then_inc(hh_out, 1)
                dve.wait_ge(hh_out, RB * c + m + 1)
                v.tensor_tensor(hl[j][:], rl[m % 2][:], hh[j][:].bitcast(F32), ALU.subtract).then_inc(split_out, 1)

            def weigh(c, e):
                dve.wait_ge(down_done, SH + RB * c + HB * (e + 1))
                wait(dve, acc_out, E * c + e - 1)
                v.scalar_tensor_tensor(out=tmp[e % 2][:], in0=ps[:, 4 + e % 3, :], scalar=cols[:, EB2 + e:EB2 + e + 1],
                                       in1=cb[:, e, bass.ts(c, CH)], op0=ALU.add, op1=ALU.mult).then_inc(tmp_out, 1)

            def store(c):
                dve.wait_ge(finT_full, c + 1)
                wait(dve, out_st, 16 * c)
                v.tensor_tensor(outs[:], MI[:].rearrange("p (t d) -> p t d", d=D),
                                xa[:, bass.ts(c, CH // P), :], ALU.add).then_inc(outs_out, 1)

            last_x1(B - 2)
            normedT(B - 2)
            for n in range(0, 3):
                split_shared(n)
            last_x1(B - 1)
            for n in range(3, YT_AT):
                split_shared(n)
            normedT(B - 1)
            for n in range(YT_AT, LOGITS_AT):
                split_shared(n)
            dve.wait_ge(nexp, 1)
            ch.step(v.tensor_scalar(pr[:], pr[:], 1.0, None, ALU.add))
            ch.step(v.reciprocal(pr[:], pr[:]))
            v.tensor_tensor(rk[0][:], pr[:].unsqueeze(2).broadcast_to([P, NT, E, E]),
                            pr[:].unsqueeze(3).broadcast_to([P, NT, E, E]), ALU.is_equal).then_inc(equal_out, 1)
            split_shared(LOGITS_AT)
            ch.step(v.tensor_tensor(rk[1][:], pr[:].unsqueeze(2).broadcast_to([P, NT, E, E]),
                                    pr[:].unsqueeze(3).broadcast_to([P, NT, E, E]), ALU.is_gt))
            for n in range(LOGITS_AT + 1, TIES_AT):
                split_shared(n)
            dve.wait_ge(ties_out, 1)
            ch.step(v.tensor_tensor(rk[1][:], rk[1][:], rk[0][:], ALU.add))
            split_shared(TIES_AT)
            ch.step(v.tensor_reduce(rank[:], rk[1][:], AX, ALU.add))
            ch.step(v.scalar_tensor_tensor(out=comb[:], in0=rank[:], scalar=1.5, in1=pr[:], op0=ALU.is_lt, op1=ALU.mult))
            split_shared(TIES_AT + 1)
            ch.step(v.tensor_reduce(den[:], comb[:], AX, ALU.add))
            ch.step(v.tensor_scalar(den[:], den[:], 1e-6, None, ALU.add))
            ch.step(v.reciprocal(den[:], den[:]))
            v.tensor_tensor(comb[:], comb[:], den[:].unsqueeze(2).broadcast_to([P, NT, E]), ALU.mult).then_inc(comb_done, 1)
            for n in range(TIES_AT + 2, SH):
                split_shared(n)

            for m in range(RB):
                split(0, m)
                if m in (14, 16, 18):
                    if m == 14:
                        dve.wait_ge(cb_in0, 16)
                    if m == 16:
                        dve.wait_ge(comb_st, 32)
                    weigh(0, m // 2 - 7)
                if m % HB == 3 and m // HB >= 4:
                    weigh(0, m // HB - 1)
            dve.wait_ge(cb_in1, 16 * (NC - 1))
            with dve.Fori(1, NC) as c:
                for m in range(RB):
                    split(c, m)
                    if m == 3:
                        weigh(c - 1, E - 1)
                    elif m % HB == 3:
                        weigh(c, m // HB - 1)
                    if m == 9:
                        store(c - 1)
            weigh(NC - 1, E - 1)
            store(NC - 1)


_INS = ['x', 'ctx_512', 'L0_xattn_Wq', 'L0_xattn_bq', 'L0_xattn_Wk', 'L0_xattn_bk', 'L0_xattn_Wv', 'L0_xattn_bv',
        'L0_ffn_norm_weight', 'L0_ffn_router_w', 'L0_ffn_sw1', 'L0_ffn_sb1', 'L0_ffn_sw2', 'L0_ffn_sb2',
        'L0_ffn_ew1', 'L0_ffn_eb1', 'L0_ffn_ew2', 'L0_ffn_eb2']
_OUTS = [((8, 256, 128), 'float32')]


def kernel(**inputs):
    import numpy as _np
    import concourse.bacc as _bacc
    from concourse import mybir as _mybir
    from concourse.bass_utils import run_bass_kernel_spmd as _run

    nc = _bacc.Bacc("TRN2", target_bir_lowering=False, num_devices=1)
    arrays, args = {}, []
    for name in _INS:
        a = _np.ascontiguousarray(inputs[name])
        arrays[f"in_{name}_dram"] = a
        args.append(nc.dram_tensor(f"in_{name}_dram", a.shape, _mybir.dt.from_np(a.dtype), kind="ExternalInput").ap())
    for i, (shape, dtype) in enumerate(_OUTS):
        dt = _mybir.dt.from_np(_np.dtype(dtype))
        args.append(nc.dram_tensor(f"out_{i}_dram", shape, dt, kind="ExternalOutput").ap())
    xattn_moe_kernel(nc, *args)
    r = _run(nc, [arrays], core_ids=[0])
    got = tuple(r.results[0][f"out_{i}_dram"] for i in range(len(_OUTS)))
    return got[0]
```

```python
from contextlib import ExitStack

import concourse.bass as bass
from concourse import mybir

F32 = mybir.dt.float32
F32R = mybir.dt.float32r
ALU = mybir.AluOpType
ACT = mybir.ActivationFunctionType
AX = mybir.AxisListType.X

P = 128


def wait(eng, sem, value):
    if not (isinstance(value, int) and value <= 0):
        eng.wait_ge(sem, value)


class Chain:

    def __init__(self, eng, sem):
        self.eng, self.sem, self.base, self.n = eng, sem, 0, 0

    def step(self, ins):
        ins.then_inc(self.sem, 1)
        self.n += 1
        self.eng.wait_ge(self.sem, self.base + self.n)

    def enter(self, i, per_round):
        self.first, self.per_round = self.n, per_round
        self.base = (i - 1) * per_round

    def leave(self, rounds):
        assert self.n == self.first + self.per_round, (self.n - self.first, self.per_round)
        self.base, self.n = 0, self.first + rounds * self.per_round


def xattn_moe_kernel(nc, x, ctx, Wq, bq, Wk, bk, Wv, bv, nw, router_w, sw1, sb1, sw2, sb2,
                     ew1, eb1, ew2, eb2, out):
    B, LQ, D = x.shape
    NK, KD = ctx.shape[1:]
    E, _, H = ew1.shape
    T = B * LQ
    NT = T // P
    HB = H // P
    KT = NK // P
    TAIL = NK - KT * P
    TAILE = TAIL + TAIL % 2
    NKT = KT + 1
    NE = E + 1
    CH = 512
    NC = T // CH
    SH = NC * HB
    TOPK = 2
    KJ = TOPK * NT
    SLT = TOPK * T // P + E - 1
    G = 6
    SLG = (SLT + 2 + G - 1) // G
    SLW = SLT + SLT % 2
    NCOL = HB + 4
    PAIRS = B // 2
    assert D == P and NT == 16 and E <= 8 and G % 2 == 0 and LQ == 2 * P and 2 * KD == P and T % CH == 0 and B % 2 == 0

    GROUPS = [(a, min(a + 4, NKT)) for a in range(0, NKT, 4)]
    NG = len(GROUPS)

    def tile_rows(j):
        return P if j < KT else TAIL

    xt = x.rearrange("b (s p) d -> p (b s) d", p=P)
    ot = out.rearrange("b (s p) d -> p (b s) d", p=P)
    yn_d = nc.dram_tensor("normed_scratch", (T + 1, D), F32, kind="Internal").ap()
    eo_d = nc.dram_tensor("expert_out_scratch", (TOPK * T + SLT * P, D), F32, kind="Internal").ap()

    with ExitStack() as st:
        def sb(name, shape, dt=F32, ctx_=None):
            return (ctx_ or st).enter_context(nc.sbuf_tensor(name, shape, dt))

        def sem(name):
            return st.enter_context(nc.semaphore(name))

        xa = sb("xa", [P, NT, D])
        xTh = sb("xTh", [P, T], F32R)
        xTl = sb("xTl", [P, T], F32R)
        W = sb("W", [P, 2, NE, 2 * H], F32R)
        Wh, Wl = W[:, 0], W[:, 1]
        ident = sb("ident", [P, P])
        cols = sb("cols", [P, NCOL])
        B1, BQ, BK, NW, SB2 = 0, HB, HB + 1, HB + 2, HB + 3
        sharedT = sb("sharedT", [P, T])
        rwTh = sb("rwTh", [P, E], F32R)
        rwTl = sb("rwTl", [P, E], F32R)

        ph1 = ExitStack()
        craw = [sb(f"craw{u}", [P, NKT, KD], F32, ph1) for u in range(2)]
        cnat = sb("cnat", [P, NKT, 2 * KD], F32R, ph1)
        cT = [sb(f"cT{u}", [P, KT * P + TAILE], F32R, ph1) for u in range(2)]
        probs = [sb(f"probs{s}", [P, NK + NK % 2], F32, ph1) for s in range(2)]
        cpv = [sb(f"cpv{u}", [P, NKT, KD], F32, ph1) for u in range(2)]
        pT = [sb(f"pT{u}", [P, NKT, LQ], F32, ph1) for u in range(2)]
        wraw = [sb(f"wraw{u}", [P, 2 * H], F32, ph1) for u in range(2)]
        zrow = sb("zrow", [1, D], F32, ph1)
        xn = sb("xn", [P, 2, D], F32, ph1)
        yn = sb("yn", [P, 2, D], F32, ph1)
        xnT = sb("xnT", [P, LQ], F32, ph1)
        qh = [sb(f"qh{u}", [P, LQ], F32R, ph1) for u in range(2)]
        ql = [sb(f"ql{u}", [P, LQ], F32R, ph1) for u in range(2)]
        oT = sb("oT", [KD, LQ], F32, ph1)
        st6 = sb("st6", [P, NT, 6], F32, ph1)
        st6b = sb("st6b", [P, 2, 6], F32, ph1)
        mv1 = sb("mv1", [P, NT, 2], F32, ph1)
        rstd1 = sb("rstd1", [P, 2, NT], F32, ph1)
        mv2 = sb("mv2", [P, 2, 2], F32, ph1)
        lnt = sb("lnt", [P, 8, 2], F32, ph1)
        mhalf = sb("mhalf", [P, NT], F32, ph1)
        eps1 = sb("eps1", [P, NT], F32, ph1)
        eps2 = sb("eps2", [P, 2], F32, ph1)
        mx = sb("mx", [P, 4], F32, ph1)
        nbias = [sb(f"nbias{s}", [P, 1], F32, ph1) for s in range(2)]
        rsum = [sb(f"rsum{u}", [P, 2, 2], F32, ph1) for u in range(2)]
        rinv = sb("rinv", [P, 2, 2], F32, ph1)
        cq = [sb(f"cq{u}", [P, 2], F32, ph1) for u in range(2)]
        rows = sb("rows", [NCOL, P], F32, ph1)
        wq_s = sb("wq_s", [P, D], F32, ph1)
        wk_s = sb("wk_s", [KD, D], F32, ph1)
        wv_s = sb("wv_s", [KD, D], F32, ph1)
        rw_s = sb("rw_s", [E, D], F32, ph1)
        bvB = sb("bvB", [P, D], F32, ph1)
        wqT = sb("wqT", [P, D], F32, ph1)
        wk2T = sb("wk2T", [P, 2 * KD + 1], F32, ph1)
        wqk = sb("wqk", [P, 2 * KD + 1], F32, ph1)
        rwT = sb("rwT", [P, E], F32, ph1)
        bqk = sb("bqk", [P, 2], F32, ph1)
        bqrep = sb("bqrep", [P, P], F32, ph1)
        ph1.close()
        pr = sb("pr", [P, NT, E])
        rank = sb("rank", [P, NT, E])
        lowi = sb("lowi", [P, E, E])
        low128 = sb("low128", [P, E, E])
        rl = [sb(f"rl{i}", [P, CH]) for i in range(2)]
        hh = [sb(f"hh{j}", [P, CH], F32R) for j in range(HB)]
        hl = [sb(f"hl{j}", [P, CH], F32R) for j in range(HB)]
        rk = [sb(f"rk{i}", [P, NT, E, E]) for i in range(2)]
        both = sb("both", [P, NT, E], F32R)
        first = sb("first", [P, NT, E])
        PAD = NT // 2
        sums = [sb(f"sums{i}", [P, PAD + NT, E]) for i in range(4)]
        before = sb("before", [P, NT, E], F32R)
        msum = sb("msum", [P, E], F32R)
        cw = [sb(f"cw{i}", [P, NT, E]) for i in range(3)]
        wts = sb("wts", [P, TOPK, NT])
        den = sb("den", [P, NT])
        cmp16 = sb("cmp16", [P, E, NT])
        cmpE = sb("cmpE", [P, E, E])
        ntile = sb("ntile", [P, E])
        off = sb("off", [P, 2, E])
        slot = sb("slot", [P, TOPK, NT])
        sloti = sb("sloti", [P, 2, TOPK, NT], mybir.dt.int32)
        slo = sb("slo", [P, TOPK, NT])
        shi = sb("shi", [P, TOPK, NT])
        inv = [sb(f"inv{i}", [P, SLW]) for i in range(5)]
        cmpT = sb("cmpT", [1, SLT, E])
        texp = sb("texp", [1, SLT])
        upper = [sb("upper", [P, P]), sb("upperR", [P, P], F32R)]
        ones = [sb("ones", [P, P]), sb("onesR", [P, P], F32R)]
        io1 = sb("io1", [P, P])
        io128 = sb("io128", [P, SLW])
        iden = sb("iden", [P, KJ])
        junk = sb("junk", [P, SLW])
        ixg = sb("ixg", [P, SLW], mybir.dt.uint32)
        ixs = sb("ixs", [P, SLW], mybir.dt.uint32)
        epad = sb("epad", [1, SLG + 1, G])
        eights = sb("eights", [1, G + 2])
        epack = [sb("epack", [1, SLG, G]), sb("epack2", [1, SLG, 2]), sb("epack3", [1, 2, SLG])]
        expert_of = sb("expert_of", [1, SLG], mybir.dt.int32)
        row_in = [sb(f"row_in{i}", [P, 1], mybir.dt.uint32) for i in range(2)]
        row_out = [sb(f"row_out{i}", [P, 1], mybir.dt.uint32) for i in range(2)]
        xg = [sb(f"xg{i}", [P, D]) for i in range(2)]
        txh = [sb(f"txh{i}", [P, P], F32R) for i in range(2)]
        txl = [sb(f"txl{i}", [P, P], F32R) for i in range(2)]
        ylo = [sb(f"ylo{i}", [P, D]) for i in range(2)]
        ysb = [sb(f"ysb{i}", [P, D]) for i in range(2)]
        b1B = sb("b1B", [P, E, H])
        b2s = sb("b2s", [E, D])
        combT = sb("combT", [E, T])
        ph2 = ExitStack()
        hot_lo = sb("hot_lo", [P, KJ, P], F32R, ph2)
        hot = sb("hot", [P, KJ, SLW], F32, ph2)
        hot_id = sb("hot_id", [P, KJ, SLW], F32R, ph2)
        ph2.close()
        eo = sb("eo", [P, TOPK, NT, D])

        ps = st.enter_context(nc.psum_tensor("ps", [P, 8, 512], F32))
        S = ps[:, 0:4, :].rearrange("p a b -> p (a b)")
        PT = [ps[:, 4, :], ps[:, 5, :]]
        PV = ps[0:KD, 6, 0:LQ]
        MI = ps[:, 7, :]

        x_in0, x_in1, setup_in = sem("x_in0"), sem("x_in1"), sem("setup_in")
        ctx_in = [sem("ctx_in0"), sem("ctx_in1")]
        cpv_in = [sem("cpv_in0"), sem("cpv_in1")]
        w_in = [sem("w_in0"), sem("w_in1")]
        consts = sem("consts")
        setT, setT_out = sem("setT"), sem("setT_out")
        setM, setM_out = sem("setM"), sem("setM_out")
        c_hi, w_hi = sem("c_hi"), sem("w_hi")
        c_split = sem("c_split")
        w_split = sem("w_split")
        pool_chain, dve_chain = sem("pool_chain"), sem("dve_chain")
        stats1, stats2_out = sem("stats1"), sem("stats2_out")
        ln1, ln2 = sem("ln1"), sem("ln2")
        cT_full, cT_out = sem("cT_full"), sem("cT_out")
        xnT_full, xnT_out = sem("xnT_full"), sem("xnT_out")
        q_full, qh_out, q_out = sem("q_full"), sem("qh_out"), sem("q_out")
        s_done = sem("s_done")
        bias_done = sem("bias_done")
        exp_done = sem("exp_done")
        pt_full = sem("pt_full")
        pt0_out, pt1_out = sem("pt0_out"), sem("pt1_out")
        pv_done, oT_out = sem("pv_done"), sem("oT_out")
        o_done, x1_out = sem("o_done"), sem("x1_out")
        yT_full, yTh_out, yT_out = sem("yT_full"), sem("yTh_out"), sem("yT_out")
        lg_full = sem("lg_full")
        xb_out, bqk_out, rinv_out = sem("xb_out"), sem("bqk_out"), sem("rinv_out")
        nexp, sel_out, pos_full, slots_out = sem("nexp"), sem("sel_out"), sem("pos_full"), sem("slots_out")
        hot_out, hot_id_out, inv_full, tables = sem("hot_out"), sem("hot_id_out"), sem("inv_full"), sem("tables")
        equal_out, ties_out = sem("equal_out"), sem("ties_out")
        iotas, iotas_r = sem("iotas"), sem("iotas_r")
        yn_st, bias_in, eo_in = sem("yn_st"), sem("bias_in"), [sem(f"eo_in{c}") for c in range(4)]
        up_done, relu_out, split_out = sem("up_done"), sem("relu_out"), sem("split_out")
        down_done = sem("down_done")
        shared_out, sT_full = sem("shared_out"), sem("sT_full")
        rows_out = sem("rows_out")
        gathered, scattered = [sem("gathered0"), sem("gathered1")], [sem("scattered0"), sem("scattered1")]
        tx_full, txh_out, txl_out, tup_full, tup_out = sem("tx_full"), sem("txh_out"), sem("txl_out"), sem("tup_full"), sem("tup_out")
        th_full, thh_out, thl_out, td_full, ty_half, ty_out = sem("th_full"), sem("thh_out"), sem("thl_out"), sem("td_full"), sem("ty_half"), sem("ty_out")
        combT_full, combT_out = sem("combT_full"), sem("combT_out")
        wts_out, weighed0, weighed1 = sem("wts_out"), sem("weighed0"), sem("weighed1")
        comb_out, out_st = sem("comb_out"), sem("out_st")

        def there(i):
            return not isinstance(i, int) or 0 <= i < SLT

        def experts(eng, h):
            v = eng.value_load(expert_of[0:1, bass.ts(h, 1)], min_val=0, max_val=8 ** (G + 2) - 1)
            return {f: eng.snap((v // 8 ** (f + 2)) % 8 if f > -2 else v % 8, min_val=0, max_val=E - 1) for f in range(-2, G)}

        def slot_tiles(eng, cycle, load=True):
            def group(h):
                e = experts(eng, h) if load else {}
                for n in range(G):
                    cycle(G * h + n, n % 2, {-2: e.get(n - 2), 0: e.get(n)}, G // 2 * h + n // 2)
            group(0)
            with eng.Fori(1, (SLT - 3) // G) as h:
                group(h)
            for h in range((SLT - 3) // G, SLG):
                group(h)

        PROJECT_AT, ROUTER_AT, YT_AT, LOGITS_AT, TIES_AT, COUNTS_AT, SLOTS_AT = 0, 1, 1, 2, 4, 8, 11

        block = st.enter_context(nc.Block())

        @block.sync
        def _(sp):
            def load_keys(dst, b, done):
                nc.sync.dma_start(dst[:, 0:KT, :], ctx[b, 0:KT * P, :].rearrange("(p j) d -> p j d", j=KT)).then_inc(done, 16)
                nc.sync.dma_start(dst[0:TAIL, KT, :], ctx[b, KT * P:NK, :]).then_inc(done, 16)

            def load_weights(w1, w2, u):
                nc.sync.dma_start(wraw[u][:, 0:H], w1).then_inc(w_in[u], 16)
                nc.sync.dma_start(wraw[u][:, H:2 * H].rearrange("p (j o) -> p j o", j=HB),
                                  w2.rearrange("(j p) o -> p j o", p=P)).then_inc(w_in[u], 16)

            nc.sync.dma_start(xa[:, 0:4, :], xt[:, 0:4, :]).then_inc(x_in0, 16)
            sp.wait_ge(consts, 1)
            load_keys(craw[0], 0, ctx_in[0])
            nc.sync.dma_start(wq_s[:], Wq).then_inc(setup_in, 16)
            nc.sync.dma_start(wk_s[:], Wk).then_inc(setup_in, 16)
            nc.sync.dma_start(rows[0:HB, :], sb1.rearrange("(j p) -> j p", p=P)).then_inc(setup_in, 16)
            for r, v in ((BQ, bq), (BK, bk), (NW, nw), (SB2, sb2)):
                nc.sync.dma_start(rows[r:r + 1, :], v.rearrange("(a p) -> a p", a=1)).then_inc(setup_in, 16)
            nc.sync.dma_start(rw_s[:], router_w).then_inc(setup_in, 16)
            nc.sync.dma_start(wv_s[:], Wv).then_inc(setup_in, 16)
            nc.sync.dma_start(bvB[:], bv.partition_broadcast(P)).then_inc(setup_in, 16)
            nc.sync.dma_start(yn_d[T:T + 1, :], zrow[:]).then_inc(bias_in, 16)
            load_keys(craw[1], 1, ctx_in[1])
            nc.sync.dma_start(xa[:, 4:NT, :], xt[:, 4:NT, :]).then_inc(x_in1, 16)
            load_weights(sw1, sw2, 0)
            load_weights(ew1[0], ew2[0], 1)
            load_keys(cpv[0], 0, cpv_in[0])
            load_keys(cpv[1], 1, cpv_in[1])

            def store_normed(b):
                sp.wait_ge(ln2, b + 1)
                nc.sync.dma_start(yn_d[bass.ts(b, LQ), :].rearrange("(s p) d -> p s d", p=P), yn[:]).then_inc(yn_st, 16)

            def batch(b, u, last):
                if not last:
                    wait(sp, c_split, b + 1)
                    load_keys(craw[u], b + 2, ctx_in[u])
                if not (isinstance(b, int) and b < 2):
                    store_normed(b - 2)
                if not (last and u == 1):
                    wait(sp, w_split, b + 1)
                    load_weights(ew1[b + 1], ew2[b + 1], u)
                if not (isinstance(b, int) and (b == 0 or b == B - 1)):
                    wait(sp, pv_done, b)
                    load_keys(cpv[1 - u], b + 1, cpv_in[1 - u])

            batch(0, 0, False)
            batch(1, 1, False)
            with sp.Fori(1, PAIRS - 1) as i:
                batch(2 * i, 0, False)
                batch(2 * i + 1, 1, False)
            batch(B - 2, 0, True)
            batch(B - 1, 1, True)

            store_normed(B - 2)
            store_normed(B - 1)
            sp.wait_ge(x1_out, B)
            nc.sync.dma_start(b1B[:], eb1.partition_broadcast(P)).then_inc(bias_in, 16)
            nc.sync.dma_start(b2s[:], eb2).then_inc(bias_in, 16)
            sp.wait_ge(scattered[0], 16 * ((SLT + 1) // 2))
            sp.wait_ge(scattered[1], 16 * (SLT // 2))
            for c in range(4):
                for k in range(TOPK):
                    t = slice(c * NT // 4, (c + 1) * NT // 4)
                    nc.sync.dma_start(eo[:, k, t, :], eo_d[k * T:(k + 1) * T, :].rearrange(
                        "(t p) d -> p t d", p=P)[:, t, :]).then_inc(eo_in[c], 16)
            for c in range(4):
                t = slice(c * NT // 4, (c + 1) * NT // 4)
                sp.wait_ge(comb_out, c + 1)
                nc.sync.dma_start(ot[:, t, :], xa[:, t, :]).then_inc(out_st, 16)
            sp.wait_ge(out_st, 16 * 4)

        @block.gpsimd
        def _(pool):
            ch = Chain(pool, pool_chain)
            gp = nc.gpsimd

            gp.memset(zrow[:], 0.0)
            gp.memset(craw[0][:, KT, :], 0.0)
            gp.memset(craw[1][:, KT, :], 0.0).then_inc(consts, 1)
            ch.step(gp.memset(ident[:], 0.0))
            gp.affine_select(out=ident[:], in_=ident[:], compare_op=ALU.not_equal, fill=1.0, base=0,
                             pattern=[[-1, P]], channel_multiplier=1).then_inc(consts, 1)
            gp.memset(eps1[:], 1e-5)
            gp.memset(eps2[:], 1e-8)
            ch.step(gp.memset(mhalf[:], -0.5))

            def split_ctx(b, k):
                pool.wait_ge(c_hi, b + 1)
                gp.tensor_tensor(cnat[:, :, KD:2 * KD], craw[k][:], cnat[:, :, 0:KD].bitcast(F32),
                                 ALU.subtract).then_inc(c_split, 1)

            def split_weights(n, e, u):
                pool.wait_ge(w_hi, n + 1)
                gp.tensor_tensor(Wl[:, e, :], wraw[u][:], Wh[:, e, :].bitcast(F32), ALU.subtract).then_inc(w_split, 1)

            def norm1(b):
                wait(pool, xnT_full, b)
                t = bass.ts(b, 2)
                ch.step(gp.tensor_tensor(xn[:], xa[:, t, :], mv1[:, t, 0:1].broadcast_to([P, 2, D]), ALU.subtract))
                gp.tensor_tensor(xn[:], xn[:], rstd1[:, 1, t].unsqueeze(2).broadcast_to([P, 2, D]),
                                 ALU.mult).then_inc(ln1, 1)
                gp.tensor_tensor(xa[:, t, :], xa[:, t, :],
                                 bvB[:].unsqueeze(1).broadcast_to([P, 2, D]), ALU.add).then_inc(xb_out, 1)

            def norm2(b):
                pool.wait_ge(stats2_out, b + 1)
                wait(pool, yT_full, b)
                wait(pool, yn_st, b * 16)
                gp.tensor_tensor(lnt[:, 2, :], mv2[:, :, 1], eps1[:, 0:2], ALU.add)
                ch.step(gp.tensor_tensor(yn[:], xa[:, bass.ts(b, 2), :],
                                         mv2[:, :, 0].unsqueeze(2).broadcast_to([P, 2, D]), ALU.subtract))
                ch.step(gp.tensor_tensor(lnt[:, 3, :], lnt[:, 2, :], mhalf[:, 0:2], ALU.pow))
                ch.step(gp.tensor_tensor(lnt[:, 4, :], mv2[:, :, 1], lnt[:, 3, :], ALU.mult))
                ch.step(gp.tensor_tensor(lnt[:, 5, :], lnt[:, 4, :], lnt[:, 3, :], ALU.mult))
                ch.step(gp.tensor_tensor(lnt[:, 6, :], lnt[:, 5, :], eps2[:], ALU.add))
                ch.step(gp.tensor_tensor(lnt[:, 7, :], lnt[:, 6, :], mhalf[:, 0:2], ALU.pow))
                ch.step(gp.tensor_tensor(lnt[:, 0, :], lnt[:, 7, :], lnt[:, 3, :], ALU.mult))
                gp.tensor_tensor(yn[:], yn[:], lnt[:, 0, :].unsqueeze(2).broadcast_to([P, 2, D]),
                                 ALU.mult).then_inc(ln2, 1)

            def rstd(t):
                ch.step(gp.tensor_tensor(rstd1[:, 0, t], mv1[:, t, 1], eps1[:, t], ALU.add))
                ch.step(gp.tensor_tensor(rstd1[:, 1, t], rstd1[:, 0, t], mhalf[:, t], ALU.pow))

            pool.wait_ge(stats1, 1)
            rstd(slice(0, 4))
            split_ctx(0, 0)
            pool.wait_ge(setup_in, 16 * 10)
            norm1(0)
            split_ctx(1, 1)
            norm1(1)
            pool.wait_ge(stats1, 2)
            rstd(slice(4, NT))

            def cycle(b, k):
                if not (isinstance(b, int) and b >= B - 2):
                    norm1(b + 2)
                if not (isinstance(b, int) and b < 2):
                    norm2(b - 2)
                split_weights(b, E if isinstance(b, int) and b == 0 else b - 1, k)
                if not (isinstance(b, int) and b >= B - 2):
                    split_ctx(b + 2, k)

            cycle(0, 0)
            cycle(1, 1)
            with pool.Fori(1, PAIRS - 1) as i:
                ch.enter(i, 2 * (1 + 7))
                cycle(2 * i, 0)
                cycle(2 * i + 1, 1)
            ch.leave(PAIRS - 2)
            cycle(B - 2, 0)
            cycle(B - 1, 1)
            split_weights(B, B - 1, 0)
            norm2(B - 2)
            norm2(B - 1)
            for dst, fill in ((lowi, 1.0), (low128, float(P))):
                ch.step(gp.memset(dst[:], fill))
                ch.step(gp.affine_select(out=dst[:], in_=dst[:], compare_op=ALU.is_gt, fill=0.0, base=0,
                                         pattern=[[1, E], [-1, E]], channel_multiplier=0))
            for f in range(G + 2):
                gp.memset(eights[:, f:f + 1], float(8 ** f))
            for i in range(4):
                gp.memset(sums[i][:, 0:PAD], 0.0)
            gp.memset(epad[:], 0.0)
            gp.memset(ones[0][:], 1.0)
            ch.step(gp.memset(upper[0][:], 1.0))
            gp.affine_select(out=upper[0][:], in_=upper[0][:], compare_op=ALU.is_gt, fill=0.0, base=0,
                             pattern=[[1, P]], channel_multiplier=-1)
            gp.iota(io1[:], pattern=[[1, P]], base=0, channel_multiplier=0, allow_small_or_imprecise_dtypes=True)
            gp.iota(io128[:], pattern=[[P, SLW]], base=0, channel_multiplier=0, allow_small_or_imprecise_dtypes=True)
            gp.iota(iden[:], pattern=[[P, KJ]], base=1, channel_multiplier=1, allow_small_or_imprecise_dtypes=True)
            gp.iota(junk[:], pattern=[[P, SLW]], base=TOPK * T + 1, channel_multiplier=1,
                    allow_small_or_imprecise_dtypes=True).then_inc(iotas, 1)
            pool.wait_ge(split_out, LOGITS_AT)
            for n in range(LOGITS_AT, SH):
                if n == TIES_AT:
                    pool.wait_ge(equal_out, 1)
                    gp.tensor_tensor(rk[0][:], rk[0][:], lowi[:].unsqueeze(1).broadcast_to([P, NT, E, E]),
                                     ALU.mult).then_inc(ties_out, 1)
                if n == SLOTS_AT:
                    pool.wait_ge(hot_out, 1)
                    gp.tensor_tensor(hot_id[:], hot[:], iden[:].unsqueeze(2).broadcast_to([P, KJ, SLW]),
                                     ALU.mult).then_inc(hot_id_out, 1)
                pool.wait_ge(relu_out, n + 1)
                gp.tensor_tensor(hl[n % HB][:], rl[n % 2][:], hh[n % HB][:].bitcast(F32),
                                 ALU.subtract).then_inc(split_out, 1)

            def gather(q):
                gp.indirect_dma_start(xg[q][:], None, yn_d, bass.IndirectOffsetOnAxis(row_in[q][:], 0)).then_inc(gathered[q], 16)

            def scatter(q):
                gp.indirect_dma_start(eo_d, bass.IndirectOffsetOnAxis(row_out[q][:], 0), ysb[q][:], None).then_inc(scattered[q], 16)

            def cycle(i, q, e, h):
                if there(i + 2):
                    pool.wait_ge(rows_out, i + 3)
                    gp.nop(nofuse=True)
                    gather(q)
                if there(i - 3):
                    pool.wait_ge(ty_out, i - 2)
                    gp.nop(nofuse=True)
                    scatter(1 - q)

            pool.wait_ge(yn_st, 16 * B)
            pool.wait_ge(bias_in, 16 * 3)
            pool.wait_ge(rows_out, 2)
            gather(0)
            gather(1)
            slot_tiles(pool, cycle, load=False)

            pool.wait_ge(wts_out, 1)
            for c in range(4):
                pool.wait_ge(eo_in[c], 32)
                t = slice(c * NT // 4, (c + 1) * NT // 4)
                gp.tensor_tensor(eo[:, 1, t, :], eo[:, 1, t, :],
                                 wts[:, 1, t].unsqueeze(2).broadcast_to([P, NT // 4, D]), ALU.mult).then_inc(weighed1, 1)

        @block.scalar
        def _(act):
            a = nc.scalar

            act.wait_ge(setT, 4)
            a.copy(wqT[:], ps[:, 0, 0:D]).then_inc(setT_out, 1)
            a.copy(cols[:], ps[:, 2, 0:NCOL]).then_inc(setT_out, 1)
            a.copy(rwT[:], ps[:, 3, 0:E]).then_inc(setT_out, 1)
            act.wait_ge(setM, 3)
            a.copy(wqk[:], ps[:, 0, 0:2 * KD + 1]).then_inc(setM_out, 1)

            def ctx_groups(b, k, gs):
                for g in gs:
                    j0, j1 = GROUPS[g]
                    act.wait_ge(cT_full, NG * b + g + 1)
                    w = (j1 - j0) * P if j1 <= KT else TAILE
                    a.copy(cT[k][:, j0 * P:j0 * P + w], PT[g % 2][:, 0:w]).then_inc(cT_out, 1)

            def queriesT(b):
                act.wait_ge(xnT_full, b + 1)
                a.copy(xnT[:], MI[:, 0:LQ]).then_inc(xnT_out, 1)

            def queries(b, k):
                act.wait_ge(q_full, b + 1)
                a.activation(qh[k][:], MI[:, 0:LQ], ACT.Identity, bias=bqk[:, 0:1]).then_inc(qh_out, 1)

            def ctx_hi(b, k):
                wait(act, ctx_in[k], (b + (2 - k)) * 16)
                wait(act, cT_full, NG * b)
                a.copy(cnat[:, :, 0:KD], craw[k][:]).then_inc(c_hi, 1)

            def weights_hi(n, e, u):
                wait(act, w_in[u], (n + (2 - u)) * 16)
                a.copy(Wh[:, e, :], wraw[u][:]).then_inc(w_hi, 1)

            def exps(g, k, s):
                act.wait_ge(bias_done, g + 1)
                a.activation(probs[s][:, 0:1024], S[:, 0:1024], ACT.Exp, bias=nbias[s][:],
                             accum_out=rsum[k][:, s, 0:1]).then_inc(exp_done, 1)
                a.activation(probs[s][:, 1024:NK], S[:, 1024:NK], ACT.Exp, bias=nbias[s][:],
                             accum_out=rsum[k][:, s, 1:2]).then_inc(exp_done, 1)

            def prob_groups(b, k, ns):
                for n in ns:
                    j0, j1 = GROUPS[n]
                    act.wait_ge(pt_full, NG * (2 * b + 1) + n + 1)
                    r = tile_rows(j1 - 1)
                    a.copy(pT[k][0:r, j0:j1, P:2 * P],
                           PT[n % 2][0:r, 0:(j1 - j0) * P].rearrange("p (a b) -> p a b", b=P)).then_inc(pt1_out, 1)

            def attn_out(b):
                act.wait_ge(pv_done, b + 1)
                a.copy(oT[:], PV).then_inc(oT_out, 1)

            def normedT(b):
                act.wait_ge(yT_full, b + 1)
                a.activation(xTh[:, bass.ts(b, LQ)], MI[:, 0:LQ], ACT.Copy, scale=cols[:, NW:NW + 1]).then_inc(yTh_out, 1)

            ctx_hi(0, 0)
            ctx_groups(0, 0, range(NG))
            ctx_hi(1, 1)
            act.wait_ge(bqk_out, 1)
            queriesT(0)
            queries(0, 0)
            queriesT(1)
            queries(1, 1)
            exps(0, 0, 0)

            def cycle(b, k):
                first = isinstance(b, int) and b == 0
                last = isinstance(b, int) and b == B - 1
                more = not (isinstance(b, int) and b >= B - 2)
                if not last:
                    ctx_groups(b + 1, 1 - k, (0, 1))
                exps(2 * b + 1, k, 1)
                if more:
                    queriesT(b + 2)
                if not last:
                    ctx_groups(b + 1, 1 - k, (2, 3))
                weights_hi(b, E if first else b - 1, k)
                if more:
                    queries(b + 2, k)
                prob_groups(b, k, (0, 1))
                if not last:
                    exps(2 * b + 2, 1 - k, 0)
                if more:
                    ctx_hi(b + 2, k)
                prob_groups(b, k, (2, 3))
                if not first:
                    attn_out(b - 1)
                if not (isinstance(b, int) and b < 2):
                    normedT(b - 2)

            cycle(0, 0)
            cycle(1, 1)
            with act.Fori(1, PAIRS - 1) as i:
                cycle(2 * i, 0)
                cycle(2 * i + 1, 1)
            cycle(B - 2, 0)
            cycle(B - 1, 1)
            weights_hi(B, B - 1, 0)
            attn_out(B - 1)
            normedT(B - 2)

            def relu_shared(n):
                j, bias = n % HB, cols[:, B1 + n % HB:B1 + n % HB + 1]
                act.wait_ge(up_done, n + 1)
                wait(act, down_done, n - 3)
                a.activation(hh[j][:], ps[:, j, :], ACT.Relu, bias=bias)
                wait(act, split_out, n - 1)
                a.activation(rl[n % 2][:], ps[:, j, :], ACT.Relu, bias=bias).then_inc(relu_out, 1)

            def shared(c):
                act.wait_ge(down_done, HB * (c + 1))
                a.activation(sharedT[:, c * CH:(c + 1) * CH], ps[:, 4 + c % 2, :], ACT.Identity,
                             bias=cols[:, SB2:SB2 + 1]).then_inc(shared_out, 1)

            for n in range(SH):
                relu_shared(n)
                if n % HB == HB - 1 and n > HB:
                    shared(n // HB - 1)
                if n == YT_AT:
                    normedT(B - 1)
                if n == LOGITS_AT:
                    act.wait_ge(lg_full, 1)
                    a.activation(pr[:].rearrange("p t e -> p (t e)"), ps[:, 6, 384:384 + NT * E], ACT.Exp,
                                 scale=-1.0).then_inc(nexp, 1)
            shared(NC - 1)

            def cycle(i, q, e, h):
                if there(i + 1):
                    tile_x(i + 1, 1 - q)
                if there(i - 2):
                    act.wait_ge(td_full, i - 1)
                    a.copy(ylo[q][:], ps[:, 5 + q, D:2 * D]).then_inc(ty_half, 1)
                if there(i):
                    act.wait_ge(th_full, i + 1)
                    a.activation(hh[q][:], ps[:, 3 + q, :], ACT.Relu).then_inc(thh_out, 1)

            def tile_x(i, q):
                act.wait_ge(tx_full, i + 1)
                wait(act, tup_full, i - 1)
                a.activation(txh[q][:], ps[:, 7 * q, 0:P], ACT.Copy, scale=cols[:, NW:NW + 1]).then_inc(txh_out, 1)

            for c in range(NC):
                act.wait_ge(combT_full, c + 1)
                a.copy(combT[:, c * CH:(c + 1) * CH], ps[0:E, 1 + c, :]).then_inc(combT_out, 1)
            tile_x(0, 0)
            slot_tiles(act, cycle, load=False)

            act.wait_ge(wts_out, 1)
            for c in range(4):
                act.wait_ge(eo_in[c], 32)
                for t in range(c * NT // 4, (c + 1) * NT // 4):
                    last = a.activation(eo[:, 0, t, :], eo[:, 0, t, :], ACT.Copy, scale=wts[:, 0, t:t + 1])
                last.then_inc(weighed0, 1)

        @block.tensor
        def _(pe):
            mm, tr = nc.tensor.matmul, nc.tensor.transpose

            pe.wait_ge(consts, 2)
            pe.wait_ge(setup_in, 16 * 10)
            tr(ps[:, 0, 0:D], wq_s[:], ident[:]).then_inc(setT, 1)
            tr(ps[:, 1, 0:KD], wk_s[:], ident[0:KD, 0:KD]).then_inc(setT, 1)
            tr(ps[:, 2, 0:NCOL], rows[:], ident[0:NCOL, 0:NCOL]).then_inc(setT, 1)
            tr(ps[:, 3, 0:E], rw_s[:], ident[0:E, 0:E]).then_inc(setT, 1)
            pe.wait_ge(setT_out, 6)
            mm(ps[:, 0, 0:2 * KD + 1], wqT[:], wk2T[:], start=True, stop=True).then_inc(setM, 1)
            mm(ps[:, 1, 0:1], wk2T[:, 0:2 * KD], cols[:, BQ:BQ + 1], start=True, stop=True).then_inc(setM, 1)
            mm(ps[:, 2, 0:1], bqrep[:], cols[:, BK:BK + 1], start=True, stop=True).then_inc(setM, 1)

            def ctx_groups(b, gs):
                for g in gs:
                    j0, j1 = GROUPS[g]
                    if g == 0:
                        pe.wait_ge(c_split, b + 1)
                    if isinstance(b, int) and (b == 0 or b == 1 and g < 2):
                        wait(pe, cT_out, NG * b + g - 1)
                    elif g < 2:
                        pe.wait_ge(pt1_out, NG * (b - 1) - 1 + g)
                    else:
                        pe.wait_ge(pt0_out, NG * (b - 1) + g + 1)
                    for j in range(j0, j1):
                        r = P if j < KT else TAILE
                        last = tr(PT[g % 2][:, (j - j0) * P:(j - j0) * P + r],
                                  cnat[0:r, j, :].bitcast(F32), ident[0:r, 0:r])
                    last.then_inc(cT_full, 1)

            def queriesT(b):
                pe.wait_ge(ln1, b + 1)
                wait(pe, x1_out, b - 3)
                wait(pe, q_out, b)
                for s in range(2):
                    last = tr(MI[:, s * P:(s + 1) * P], xn[:, s, :], ident[:])
                last.then_inc(xnT_full, 1)

            def queries(b):
                pe.wait_ge(xnT_out, b + 1)
                mm(MI[:, 0:LQ], wqk[:, 0:2 * KD], xnT[:], start=True, stop=True)
                for s in range(2):
                    last = mm(MI[:, LQ + s:LQ + s + 1], xnT[:, s * P:(s + 1) * P], wqk[:, 2 * KD:2 * KD + 1],
                              start=True, stop=True)
                last.then_inc(q_full, 1)

            def scores(g, b, k, s):
                if s == 0:
                    pe.wait_ge(q_out, b + 1)
                for n, (j0, j1) in enumerate(GROUPS):
                    if n % 2 == 0:
                        wait(pe, exp_done, 2 * g - 1 + n // 2)
                    if s == 0:
                        pe.wait_ge(cT_out, NG * b + n + 1)
                    a0 = j0 * P
                    w = (j1 - j0) * P if j1 <= KT else TAILE
                    mm(S[:, a0:a0 + w], qh[k][:, s * P:(s + 1) * P], cT[k][:, a0:a0 + w], start=True, stop=False)
                    last = mm(S[:, a0:a0 + w], ql[k][:, s * P:(s + 1) * P], cT[k][:, a0:a0 + w], start=False, stop=True)
                    if n % 2 == 1:
                        last.then_inc(s_done, 1)

            def turns(b, k, s, ns):
                mine, other = (pt0_out, pt1_out) if s == 0 else (pt1_out, pt0_out)
                for n in ns:
                    j0, j1 = GROUPS[n]
                    if n % 2 == 0:
                        pe.wait_ge(exp_done, 2 * (2 * b + s) + n // 2 + 1)
                    if n >= 2:
                        pe.wait_ge(mine, NG * b + n - 1)
                    elif not (isinstance(b, int) and b == B - 1):
                        pe.wait_ge(cT_out, NG * (b + 1) + 2 * s + n + 1)
                    else:
                        pe.wait_ge(other, NG * (b + s) - 1 + n)
                    for j in range(j0, j1):
                        r = tile_rows(j)
                        last = tr(PT[n % 2][0:r, (j - j0) * P:(j - j0 + 1) * P],
                                  probs[s][:, j * P:j * P + r], ident[:])
                    last.then_inc(pt_full, 1)

            def attend(b, k, j0, j1):
                if j0 == 0:
                    pe.wait_ge(pt0_out, NG * (b + 1))
                    pe.wait_ge(pt1_out, NG * (b + 1))
                    pe.wait_ge(cpv_in[k], (b + 2 - k) * 16)
                    wait(pe, oT_out, b)
                for j in range(j0, j1):
                    r = tile_rows(j)
                    last = mm(PV, cpv[k][0:r, j, :], pT[k][0:r, j, :], start=(j == 0), stop=(j == NKT - 1))
                if j1 == NKT:
                    last.then_inc(pv_done, 1)

            def project(b):
                pe.wait_ge(oT_out, b + 1)
                wait(pe, yT_out, b)
                pe.wait_ge(q_out, min(b + 4, B) if isinstance(b, int) else b + 4)
                for s in range(2):
                    last = mm(MI[:, s * P:(s + 1) * P], oT[:, s * P:(s + 1) * P], wv_s[:], start=True, stop=True)
                last.then_inc(o_done, 1)

            def normedT(b, queries_read, projections_read):
                pe.wait_ge(ln2, b + 1)
                pe.wait_ge(q_out, queries_read)
                pe.wait_ge(x1_out, projections_read)
                wait(pe, yT_out, b)
                for s in range(2):
                    last = tr(MI[:, s * P:(s + 1) * P], yn[:, s, :], ident[:])
                last.then_inc(yT_full, 1)

            def router(t0, t1):
                for t in range(t0, t1):
                    lg, x_t = ps[:, 6, 384 + t * E:384 + (t + 1) * E], slice(t * P, (t + 1) * P)
                    mm(lg, xTh[:, x_t], rwTh[:], start=True, stop=False)
                    mm(lg, xTl[:, x_t], rwTh[:], start=False, stop=False)
                    last = mm(lg, xTh[:, x_t], rwTl[:], start=False, stop=True)
                return last

            ctx_groups(0, range(NG))
            pe.wait_ge(setM_out, 1)
            pe.wait_ge(bqk_out, 1)
            for b in range(2):
                queriesT(b)
                queries(b)
                if b == 0:
                    scores(0, 0, 0, 0)

            def cycle(b, k):
                first = isinstance(b, int) and b == 0
                last = isinstance(b, int) and b == B - 1
                more = not (isinstance(b, int) and b >= B - 2)
                later = not (isinstance(b, int) and b < 2)

                def attend_before(j0, j1):
                    if not first:
                        attend(b - 1, 1 - k, j0, j1)
                scores(2 * b + 1, b, k, 1)
                if not last:
                    ctx_groups(b + 1, (0, 1))
                attend_before(0, 2)
                if later:
                    project(b - 2)
                attend_before(2, 4)
                turns(b, k, 0, (0, 1))
                attend_before(4, 6)
                turns(b, k, 0, (2, 3))
                if more:
                    queriesT(b + 2)
                attend_before(6, 7)
                if not last:
                    ctx_groups(b + 1, (2, 3))
                    scores(2 * b + 2, b + 1, 1 - k, 0)
                if more:
                    queries(b + 2)
                turns(b, k, 1, (0, 1))
                attend_before(7, 10)
                turns(b, k, 1, (2, 3))
                attend_before(10, NKT)
                if later:
                    normedT(b - 2, b + 3 if more else B, b - 1)

            cycle(0, 0)
            cycle(1, 1)
            with pe.Fori(1, PAIRS - 1) as i:
                cycle(2 * i, 0)
                cycle(2 * i + 1, 1)
            cycle(B - 2, 0)
            cycle(B - 1, 1)
            project(B - 2)
            attend(B - 1, 1, 0, NKT)
            normedT(B - 2, B, B - 1)

            LAG = 3

            def up(n, e, j, xs):
                wait(pe, relu_out, n - 3)
                w = slice(j * P, (j + 1) * P)
                mm(ps[:, j, :], Wh[:, e, w], xTh[:, xs], start=True, stop=False)
                mm(ps[:, j, :], Wh[:, e, w], xTl[:, xs], start=False, stop=False)
                mm(ps[:, j, :], Wl[:, e, w], xTh[:, xs], start=False, stop=True).then_inc(up_done, 1)

            def down(n, e, j, y):
                pe.wait_ge(split_out, n + 1)
                w = slice(H + j * P, H + (j + 1) * P)
                mm(ps[:, y, :], Wh[:, e, w], hh[j][:], start=(j == 0), stop=False)
                mm(ps[:, y, :], Wl[:, e, w], hh[j][:], start=False, stop=False)
                last = mm(ps[:, y, :], Wh[:, e, w], hl[j][:], start=False, stop=(j == HB - 1))
                last.then_inc(down_done, 1)

            def down_shared(n):
                c = n // HB
                if n % HB == 0:
                    wait(pe, shared_out, c - 1)
                down(n, E, n % HB, 4 + c % 2)

            pos, cnt, invp = ps[:, 6, 0:NT * E], ps[:, 6, NT * E:NT * E + E], ps[:, 6, 256:256 + SLW]

            def counts():
                pe.wait_ge(iotas_r, 1)
                pe.wait_ge(sel_out, 1)
                flat = both[:].rearrange("p t e -> p (t e)")
                mm(pos, upper[1][:], flat, start=True, stop=False)
                mm(pos, ones[1][:], before[:].rearrange("p t e -> p (t e)"), start=False, stop=True)
                mm(cnt, ones[1][:], msum[:], start=True, stop=True).then_inc(pos_full, 1)

            def invert():
                pe.wait_ge(hot_id_out, 1)
                for half in range(2):
                    pe.wait_ge(slots_out, half + 1)
                    for j in range(half * KJ // 2, (half + 1) * KJ // 2):
                        last = mm(invp, hot_lo[:, j, :], hot_id[:, j, :], start=(j == 0), stop=(j == KJ - 1))
                last.then_inc(inv_full, 1)

            pe.wait_ge(w_split, NE)
            for n in range(SH):
                up(n, E, n % HB, slice(n // HB * CH, (n // HB + 1) * CH))
                if n >= LAG:
                    down_shared(n - LAG)
                if n == PROJECT_AT:
                    project(B - 1)
                if n == ROUTER_AT:
                    pe.wait_ge(yT_out, B - 1)
                    router(0, NT - 2)
                if n == YT_AT:
                    normedT(B - 1, B, B)
                if n == LOGITS_AT:
                    pe.wait_ge(yT_out, B)
                    router(NT - 2, NT).then_inc(lg_full, 1)
                if n == COUNTS_AT:
                    counts()

            for n in range(SH - LAG, SH):
                down_shared(n)
            invert()
            pe.wait_ge(wts_out, 1)
            pe.wait_ge(shared_out, NC)
            for c in range(NC):
                for t in range(CH // P):
                    last = tr(ps[0:E, 1 + c, t * P:(t + 1) * P], cw[0][:, c * CH // P + t, :], ident[:])
                last.then_inc(combT_full, 1)
            pe.wait_ge(combT_out, NC)
            pe.wait_ge(tables, 1)

            def tile_xT(i, q, n):
                pe.wait_ge(gathered[q], 16 * n)
                wait(pe, txl_out, i - 1)
                tr(ps[:, 7 * q, 0:P], xg[q][:], ident[:]).then_inc(tx_full, 1)

            def cycle(i, q, e, h):
                if there(i):
                    pe.wait_ge(txl_out, i + 1)
                    wait(pe, tup_out, i - 1)
                    y = ps[:, 1 + q, :]
                    mm(y, txh[q][:], W[:, 0, e[0], 0:H], start=True, stop=False)
                    mm(y, txl[q][:], W[:, 0, e[0], 0:H], start=False, stop=False)
                    mm(y, txh[q][:], W[:, 1, e[0], 0:H], start=False, stop=True).then_inc(tup_full, 1)
                if there(i + 1):
                    tile_xT(i + 1, 1 - q, h + 1 + q)
                if there(i - 2):
                    pe.wait_ge(thl_out, i - 1)
                    wait(pe, ty_out, i - 3)
                    for j in range(HB):
                        w, k = slice(H + j * P, H + (j + 1) * P), slice(j * P, (j + 1) * P)
                        mm(ps[:, 5 + q, 0:2 * D].rearrange("p (a d) -> p a d", a=2), hh[q][:, k], W[:, :, e[-2], w],
                           start=(j == 0), stop=False)
                        last = mm(ps[:, 5 + q, 0:D], hl[q][:, k], W[:, 0, e[-2], w], start=False, stop=(j == HB - 1))
                    last.then_inc(td_full, 1)
                if there(i):
                    pe.wait_ge(tup_out, i + 1)
                    wait(pe, thl_out, i - 1)
                    for j in range(HB):
                        last = tr(ps[:, 3 + q, j * P:(j + 1) * P], rl[q][:, j * P:(j + 1) * P], ident[:])
                    last.then_inc(th_full, 1)

            tile_xT(0, 0, 1)
            slot_tiles(pe, cycle)
            pe.wait_ge(bias_in, 16 * 3)
            pe.wait_ge(ty_out, SLT)
            for c in range(NC):
                for t in range(CH // P):
                    y, x_t = ps[:, c, t * P:(t + 1) * P], slice(c * CH + t * P, c * CH + (t + 1) * P)
                    mm(y, combT[:, x_t], b2s[:], start=True, stop=False)
                    last = mm(y, sharedT[:, x_t], ident[:], start=False, stop=True)
                last.then_inc(sT_full, 1)

        @block.vector
        def _(dve):
            v = nc.vector
            ch = Chain(dve, dve_chain)

            def stats2(b):
                for s in range(2):
                    last = v.bn_stats(st6b[:, s, :], xa[:, 2 * b + s, :])
                return last

            def moments2():
                for s in range(2):
                    last = v.bn_aggr(mv2[:, s, :], st6b[:, s, :])
                last.then_inc(stats2_out, 1)

            def stats(t0, t1):
                for t in range(t0, t1):
                    last = v.bn_stats(st6[:, t, :], xa[:, t, :])
                ch.step(last)
                for t in range(t0, t1):
                    last = v.bn_aggr(mv1[:, t, :], st6[:, t, :])
                last.then_inc(stats1, 1)

            dve.wait_ge(x_in0, 16)
            stats(0, 4)
            dve.wait_ge(setT, 4)
            v.tensor_copy(wk2T[:, 0:KD], ps[:, 1, 0:KD])
            v.tensor_copy(wk2T[:, KD:2 * KD], ps[:, 1, 0:KD]).then_inc(setT_out, 1)
            dve.wait_ge(setT_out, 4)
            v.tensor_copy(wk2T[:, 2 * KD:2 * KD + 1], cols[:, BK:BK + 1]).then_inc(setT_out, 1)
            v.tensor_copy(bqrep[:], cols[:, BQ:BQ + 1].broadcast_to([P, P])).then_inc(setT_out, 1)
            ch.step(v.tensor_copy(rwTh[:], rwT[:]))
            ch.step(v.tensor_tensor(rwTl[:], rwT[:], rwTh[:].bitcast(F32), ALU.subtract))
            dve.wait_ge(setM, 3)
            v.tensor_copy(bqk[:, 0:1], ps[:, 1, 0:1])
            v.tensor_copy(bqk[:, 1:2], ps[:, 2, 0:1]).then_inc(bqk_out, 1)
            dve.wait_ge(bqk_out, 1)

            def queries(b, k):
                dve.wait_ge(qh_out, b + 1)
                v.scalar_tensor_tensor(out=ql[k][:], in0=MI[:, 0:LQ], scalar=bqk[:, 0:1], in1=qh[k][:].bitcast(F32),
                                       op0=ALU.add, op1=ALU.subtract)
                v.tensor_scalar(cq[k][:], MI[:, LQ:LQ + 2], bqk[:, 1:2], None, ALU.add).then_inc(q_out, 1)

            def row_max(g, k, s):
                dve.wait_ge(s_done, 2 * g + 1)
                v.tensor_reduce(mx[:, 0:1], S[:, 0:1024], AX, ALU.max)
                dve.wait_ge(s_done, 2 * g + 2)
                ch.step(v.tensor_reduce(mx[:, 1:2], S[:, 1024:NK], AX, ALU.max))
                ch.step(v.scalar_tensor_tensor(out=mx[:, 2:3], in0=mx[:, 0:1], scalar=mx[:, 1:2],
                                               in1=cq[k][:, s:s + 1], op0=ALU.max, op1=ALU.add))
                v.scalar_tensor_tensor(out=nbias[s][:], in0=mx[:, 2:3], scalar=-1.0, in1=cq[k][:, s:s + 1],
                                       op0=ALU.mult, op1=ALU.add).then_inc(bias_done, 1)

            def prob_groups(b, k, ns):
                for n in ns:
                    j0, j1 = GROUPS[n]
                    dve.wait_ge(pt_full, NG * 2 * b + n + 1)
                    r = tile_rows(j1 - 1)
                    v.tensor_copy(pT[k][0:r, j0:j1, 0:P],
                                  PT[n % 2][0:r, 0:(j1 - j0) * P].rearrange("p (a b) -> p a b", b=P)).then_inc(pt0_out, 1)

            def row_sums(b, k):
                dve.wait_ge(exp_done, 4 * b + 4)
                ch.step(v.tensor_tensor(rinv[:, 0, :], rsum[k][:, :, 0], rsum[k][:, :, 1], ALU.add))
                v.reciprocal(rinv[:, 1, :], rinv[:, 0, :]).then_inc(rinv_out, 1)

            def x1(b):
                dve.wait_ge(rinv_out, b + 1)
                dve.wait_ge(xb_out, b + 1)
                dve.wait_ge(o_done, b + 1)
                for s in range(2):
                    last = v.scalar_tensor_tensor(out=xa[:, 2 * b + s, :], in0=MI[:, s * P:(s + 1) * P],
                                                  scalar=rinv[:, 1, s:s + 1], in1=xa[:, 2 * b + s, :],
                                                  op0=ALU.mult, op1=ALU.add)
                last.then_inc(x1_out, 1)
                dve.wait_ge(x1_out, b + 1)

            def normedT(b):
                dve.wait_ge(yTh_out, b + 1)
                t = bass.ts(b, LQ)
                v.scalar_tensor_tensor(out=xTl[:, t], in0=MI[:, 0:LQ], scalar=cols[:, NW:NW + 1],
                                       in1=xTh[:, t].bitcast(F32), op0=ALU.mult, op1=ALU.subtract).then_inc(yT_out, 1)

            queries(0, 0)
            row_max(0, 0, 0)
            dve.wait_ge(x_in1, 16)
            stats(4, NT)
            queries(1, 1)

            def cycle(b, k):
                later = not (isinstance(b, int) and b < 2)
                if later:
                    x1(b - 2)
                if not (isinstance(b, int) and b == 0):
                    row_sums(b - 1, 1 - k)
                if later:
                    ch.step(stats2(b - 2))
                    wait(dve, ln2, b - 2)
                prob_groups(b, k, (0,))
                if later:
                    moments2()
                prob_groups(b, k, (1, 2, 3))
                if not (isinstance(b, int) and b == B - 1):
                    row_max(2 * b + 2, 1 - k, 0)
                if not (isinstance(b, int) and b >= B - 2):
                    queries(b + 2, k)
                if not (isinstance(b, int) and b == B - 1):
                    row_max(2 * b + 3, 1 - k, 1)
                if later:
                    normedT(b - 2)

            row_max(1, 0, 1)
            cycle(0, 0)
            cycle(1, 1)
            with dve.Fori(1, PAIRS - 1) as i:
                ch.enter(i, 2 * (4 + 2))
                cycle(2 * i, 0)
                cycle(2 * i + 1, 1)
            ch.leave(PAIRS - 2)
            cycle(B - 2, 0)
            cycle(B - 1, 1)

            def last_x1(b):
                x1(b)
                if b == B - 2:
                    row_sums(B - 1, 1)
                ch.step(stats2(b))
                dve.wait_ge(ln2, b)
                moments2()

            def split_shared(n):
                dve.wait_ge(relu_out, n + 1)
                v.tensor_tensor(hl[n % HB][:], rl[n % 2][:], hh[n % HB][:].bitcast(F32),
                                ALU.subtract).then_inc(split_out, 1)

            last_x1(B - 2)
            normedT(B - 2)
            last_x1(B - 1)
            for n in range(0, YT_AT):
                split_shared(n)
            normedT(B - 1)
            for n in range(YT_AT, LOGITS_AT):
                split_shared(n)
            dve.wait_ge(nexp, 1)
            ch.step(v.tensor_scalar(pr[:], pr[:], 1.0, None, ALU.add))
            ch.step(v.reciprocal(pr[:], pr[:]))
            v.tensor_tensor(rk[0][:], pr[:].unsqueeze(2).broadcast_to([P, NT, E, E]),
                            pr[:].unsqueeze(3).broadcast_to([P, NT, E, E]), ALU.is_equal).then_inc(equal_out, 1)
            ch.step(v.tensor_tensor(rk[1][:], pr[:].unsqueeze(2).broadcast_to([P, NT, E, E]),
                                    pr[:].unsqueeze(3).broadcast_to([P, NT, E, E]), ALU.is_gt))
            dve.wait_ge(ties_out, 1)
            ch.step(v.tensor_tensor(rk[1][:], rk[1][:], rk[0][:], ALU.add))
            ch.step(v.tensor_reduce(rank[:], rk[1][:], AX, ALU.add))
            dve.wait_ge(iotas, 1)
            v.tensor_copy(upper[1][:], upper[0][:])
            v.tensor_copy(ones[1][:], ones[0][:]).then_inc(iotas_r, 1)
            v.tensor_scalar(first[:], rank[:], 0.5, None, ALU.is_lt)
            v.tensor_scalar(both[:], rank[:], 1.5, None, ALU.is_lt)
            ch.step(v.tensor_scalar(sums[0][:, PAD:], rank[:], 1.5, None, ALU.is_lt))

            def shifted(i, t):
                return sums[i][:, PAD - t:PAD - t + NT]
            ch.step(v.tensor_tensor(sums[1][:, PAD:], shifted(0, 1), shifted(0, 2), ALU.add))
            ch.step(v.tensor_tensor(sums[2][:, PAD:], shifted(1, 0), shifted(1, 2), ALU.add))
            ch.step(v.tensor_tensor(sums[3][:, PAD:], shifted(2, 0), shifted(2, 4), ALU.add))
            ch.step(v.tensor_tensor(before[:], shifted(3, 0), shifted(3, 8), ALU.add))
            v.tensor_tensor(msum[:], before[:, NT - 1, :].bitcast(F32), sums[0][:, PAD + NT - 1, :], ALU.add).then_inc(sel_out, 1)

            dve.wait_ge(pos_full, 1)
            pos, cnt, invp = ps[:, 6, 0:NT * E], ps[:, 6, NT * E:NT * E + E], ps[:, 6, 256:256 + SLW]
            ch.step(v.tensor_tensor(cmp16[:], cnt.unsqueeze(2).broadcast_to([P, E, NT]),
                                    io128[:, 0:NT].unsqueeze(1).broadcast_to([P, E, NT]), ALU.is_gt))
            ch.step(v.tensor_reduce(ntile[:], cmp16[:], AX, ALU.add))
            ch.step(v.tensor_tensor(cmpE[:], low128[:], ntile[:].unsqueeze(1).broadcast_to([P, E, E]), ALU.mult))
            ch.step(v.tensor_reduce(off[:, 0, :], cmpE[:], AX, ALU.add))
            ch.step(v.scalar_tensor_tensor(out=off[:, 1, :], in0=ntile[:], scalar=float(P), in1=off[:, 0, :],
                                           op0=ALU.mult, op1=ALU.add))
            ch.step(v.tensor_tensor(cw[0][:], pos.rearrange("p (t e) -> p t e", e=E),
                                    off[:, 0, :].unsqueeze(1).broadcast_to([P, NT, E]), ALU.add))
            ch.step(v.tensor_tensor(cw[1][:], cw[0][:], first[:], ALU.mult))
            ch.step(v.tensor_tensor(cw[2][:], cw[0][:], both[:].bitcast(F32), ALU.mult))
            v.tensor_reduce(slot[:, 0, :], cw[1][:], AX, ALU.add)
            ch.step(v.tensor_reduce(slot[:, 1, :], cw[2][:], AX, ALU.add))
            ch.step(v.tensor_tensor(slot[:, 1, :], slot[:, 1, :], slot[:, 0, :], ALU.subtract))
            ch.step(v.tensor_copy(sloti[:, 0], slot[:]))
            ch.step(v.tensor_scalar(sloti[:, 1], sloti[:, 0], P - 1, None, ALU.bitwise_and))
            ch.step(v.tensor_copy(slo[:], sloti[:, 1]))
            ch.step(v.tensor_tensor(shi[:], slot[:], slo[:], ALU.subtract))
            slo_, shi_ = slo[:].rearrange("p k t -> p (k t)"), shi[:].rearrange("p k t -> p (k t)")
            dve.wait_ge(yn_st, 16 * B)
            v.tensor_tensor(hot[:], io128[:].unsqueeze(1).broadcast_to([P, KJ, SLW]),
                            shi_.unsqueeze(2).broadcast_to([P, KJ, SLW]), ALU.is_equal).then_inc(hot_out, 1)
            for half in range(2):
                j = slice(half * KJ // 2, (half + 1) * KJ // 2)
                v.tensor_tensor(hot_lo[:, j, :], io1[:].unsqueeze(1).broadcast_to([P, KJ // 2, P]),
                                slo_[:, j].unsqueeze(2).broadcast_to([P, KJ // 2, P]), ALU.is_equal).then_inc(slots_out, 1)
            ch.step(v.tensor_tensor(cmpT[:], io128[0:1, 0:SLT].unsqueeze(2).broadcast_to([1, SLT, E]),
                                    off[0:1, 1, :].unsqueeze(1).broadcast_to([1, SLT, E]), ALU.is_ge))
            ch.step(v.tensor_reduce(texp[:], cmpT[:], AX, ALU.add))
            ch.step(v.tensor_scalar(epad[:].rearrange("a g f -> a (g f)")[:, 2:2 + SLT], texp[:], float(E - 1), None, ALU.min))
            v.tensor_tensor(epack[0][:], epad[:, 0:SLG, :], eights[:, 0:G].unsqueeze(1).broadcast_to([1, SLG, G]), ALU.mult)
            ch.step(v.tensor_tensor(epack[1][:], epad[:, 1:SLG + 1, 0:2], eights[:, G:G + 2].unsqueeze(1).broadcast_to([1, SLG, 2]), ALU.mult))
            v.tensor_reduce(epack[2][:, 0, :], epack[0][:], AX, ALU.add)
            ch.step(v.tensor_reduce(epack[2][:, 1, :], epack[1][:], AX, ALU.add))
            v.tensor_tensor(expert_of[:], epack[2][:, 0, :], epack[2][:, 1, :], ALU.add)

            ch.step(v.tensor_tensor(cw[0][:], first[:], pr[:], ALU.mult))
            ch.step(v.tensor_tensor(cw[1][:], both[:].bitcast(F32), pr[:], ALU.mult))
            v.tensor_reduce(wts[:, 0, :], cw[0][:], AX, ALU.add)
            ch.step(v.tensor_tensor(cw[2][:], cw[1][:], cw[0][:], ALU.subtract))
            ch.step(v.tensor_reduce(wts[:, 1, :], cw[2][:], AX, ALU.add))
            ch.step(v.tensor_tensor(den[:], wts[:, 0, :], wts[:, 1, :], ALU.add))
            ch.step(v.tensor_scalar(den[:], den[:], 1e-6, None, ALU.add))
            ch.step(v.reciprocal(den[:], den[:]))
            ch.step(v.tensor_tensor(wts[:], wts[:], den[:].unsqueeze(1).broadcast_to([P, TOPK, NT]), ALU.mult))
            ch.step(v.tensor_tensor(cw[2][:], both[:].bitcast(F32), first[:], ALU.subtract))
            v.tensor_tensor(cw[1][:], first[:], wts[:, 0, :].unsqueeze(2).broadcast_to([P, NT, E]), ALU.mult)
            ch.step(v.tensor_tensor(cw[2][:], cw[2][:], wts[:, 1, :].unsqueeze(2).broadcast_to([P, NT, E]), ALU.mult))
            v.tensor_tensor(cw[0][:], cw[1][:], cw[2][:], ALU.add).then_inc(wts_out, 1)

            dve.wait_ge(inv_full, 1)
            v.tensor_scalar(inv[0][:], invp, 0.5, None, ALU.is_lt)
            ch.step(v.tensor_scalar(inv[1][:], invp, T + 0.5, float(-T), ALU.is_gt, ALU.mult))
            v.scalar_tensor_tensor(out=inv[2][:], in0=inv[0][:], scalar=T + 1.0, in1=invp, op0=ALU.mult, op1=ALU.add)
            ch.step(v.tensor_tensor(inv[3][:], inv[0][:], junk[:], ALU.mult))
            v.tensor_tensor(inv[2][:], inv[2][:], inv[1][:], ALU.add)
            ch.step(v.tensor_tensor(inv[4][:], inv[3][:], invp, ALU.add))
            v.tensor_scalar(ixg[:], inv[2][:], -1.0, None, ALU.add)
            v.tensor_scalar(ixs[:], inv[4][:], -1.0, None, ALU.add).then_inc(tables, 1)

            def tile_x(i, q):
                dve.wait_ge(txh_out, i + 1)
                v.scalar_tensor_tensor(out=txl[q][:], in0=ps[:, 7 * q, 0:P], scalar=cols[:, NW:NW + 1],
                                       in1=txh[q][:].bitcast(F32), op0=ALU.mult, op1=ALU.subtract).then_inc(txl_out, 1)

            def cycle(i, q, e, h):
                if there(i):
                    dve.wait_ge(tup_full, i + 1)
                    v.tensor_tensor(rl[q][:], ps[:, 1 + q, :], b1B[:, e[0], :], ALU.add).then_inc(tup_out, 1)
                if there(i + 1):
                    tile_x(i + 1, 1 - q)
                if there(i + 3):
                    rows_in(i + 3, 1 - q)
                if there(i - 1):
                    dve.wait_ge(thh_out, i)
                    v.scalar_tensor_tensor(out=hl[1 - q][:], in0=ps[:, 4 - q, :], scalar=0.0,
                                           in1=hh[1 - q][:].bitcast(F32), op0=ALU.max, op1=ALU.subtract).then_inc(thl_out, 1)
                if there(i - 2):
                    dve.wait_ge(ty_half, i - 1)
                    wait(dve, scattered[q], 16 * (h - 1))
                    v.tensor_copy(row_out[q][:], ixs[:, bass.ts(i - 2, 1)])
                    v.tensor_tensor(ysb[q][:], ps[:, 5 + q, 0:D], ylo[q][:], ALU.add).then_inc(ty_out, 1)

            def rows_in(i, q):
                v.tensor_copy(row_in[q][:], ixg[:, bass.ts(i, 1)]).then_inc(rows_out, 1)

            dve.wait_ge(tables, 1)
            rows_in(0, 0)
            rows_in(1, 1)
            tile_x(0, 0)
            rows_in(2, 0)
            slot_tiles(dve, cycle)

            def add_shared(c):
                dve.wait_ge(sT_full, c + 1)
                t = slice(c * (CH // P), (c + 1) * (CH // P))
                ch.step(v.tensor_tensor(xa[:, t, :], ps[:, c, :].rearrange("p (t d) -> p t d", d=D), xa[:, t, :], ALU.add))
            for c in range(NC):
                add_shared(c)
            for c in range(4):
                t = slice(c * NT // 4, (c + 1) * NT // 4)
                for k, weighed in enumerate((weighed0, weighed1)):
                    dve.wait_ge(weighed, c + 1)
                    last = v.tensor_tensor(xa[:, t, :], xa[:, t, :], eo[:, k, t, :], ALU.add)
                    if k == 0:
                        ch.step(last)
                last.then_inc(comb_out, 1)


_INS = ['x', 'ctx_512', 'L0_xattn_Wq', 'L0_xattn_bq', 'L0_xattn_Wk', 'L0_xattn_bk', 'L0_xattn_Wv', 'L0_xattn_bv',
        'L0_ffn_norm_weight', 'L0_ffn_router_w', 'L0_ffn_sw1', 'L0_ffn_sb1', 'L0_ffn_sw2', 'L0_ffn_sb2',
        'L0_ffn_ew1', 'L0_ffn_eb1', 'L0_ffn_ew2', 'L0_ffn_eb2']
_OUTS = [((8, 256, 128), 'float32')]


def kernel(**inputs):
    import numpy as _np
    import concourse.bacc as _bacc
    from concourse import mybir as _mybir
    from concourse.bass_utils import run_bass_kernel_spmd as _run

    nc = _bacc.Bacc("TRN2", target_bir_lowering=False, num_devices=1)
    arrays, args = {}, []
    for name in _INS:
        a = _np.ascontiguousarray(inputs[name])
        arrays[f"in_{name}_dram"] = a
        args.append(nc.dram_tensor(f"in_{name}_dram", a.shape, _mybir.dt.from_np(a.dtype), kind="ExternalInput").ap())
    for i, (shape, dtype) in enumerate(_OUTS):
        dt = _mybir.dt.from_np(_np.dtype(dtype))
        args.append(nc.dram_tensor(f"out_{i}_dram", shape, dt, kind="ExternalOutput").ap())
    xattn_moe_kernel(nc, *args)
    r = _run(nc, [arrays], core_ids=[0])
    got = tuple(r.results[0][f"out_{i}_dram"] for i in range(len(_OUTS)))
    return got[0]
```
